# Optimizing a Trainium2 kernel written in Bass

```python
import numpy as np
import jax
import jax.numpy as jnp

def _softmax(x, axis=-1):
    return jax.nn.softmax(x, axis=axis)

def _gelu(x):
    return jax.nn.gelu(x, approximate=True)

def _silu(x):
    return jax.nn.silu(x)

def _sigmoid(x):
    return jax.nn.sigmoid(x)

def _layernorm(x, axis=-1, eps=1e-05):
    m = jnp.mean(x, axis=axis, keepdims=True)
    v = jnp.var(x, axis=axis, keepdims=True)
    return (x - m) / jnp.sqrt(v + eps)

def _scatter_add(tgt, idx, src, axis=0):
    return tgt.at[idx].add(src)

def _segment_sum(src, seg, n):
    return jax.ops.segment_sum(src, seg, n)
kernel_name = 'mk_adj_preln_d2_adj_r2_4a2ce2'

def setup_inputs(seed: int=0):
    np.random.seed(seed)
    _w = jnp.asarray

    def _rec_inputs():
        import jax
        import jax.numpy as jnp
        _gk = jax.random.key(seed)
        x = -0.0005207 + 1.001 * jax.random.normal(jax.random.fold_in(_gk, 1), (4096, 128), jnp.float32)
        _w = (1.0 + jnp.arange(4096, dtype=jnp.float32)) ** (-0.5)
        _w = _w / _w.mean()
        _pij = jnp.clip(0.000488281 * _w[:, None] * _w[None, :], 0.0, 1.0)
        _a = jax.random.uniform(jax.random.fold_in(_gk, 2), (4096, 4096)) < _pij
        adj = _a.astype(jnp.int32)
        return (x, adj)
    x, adj = _rec_inputs()

    def _L0_gnn_setup():
        import jax, jax.numpy as jnp
        import numpy as np
        ALPHA = 0.2
        MASK_VAL = -9000000000000000.0
        key = jax.random.key(seed)
        k1, k2, k3, k4 = jax.random.split(key, 4)
        N, Fin, Fout = (4096, 128, 128)
        h = jax.random.normal(k1, (N, Fin), dtype=jnp.float32)
        adj = jax.random.randint(k2, (N, N), 0, 2, dtype=jnp.int32)
        W = jax.random.normal(k3, (Fin, Fout), dtype=jnp.float32) * 0.06
        a = jax.random.normal(k4, (2 * Fout, 1), dtype=jnp.float32) * 0.06
        return {'h': h, 'adj': adj, 'W': W, 'a': a}
    _L0_gnn_all = _L0_gnn_setup()
    _L0_gnn_in = {k: v for k, v in _L0_gnn_all.items() if k in ('W', 'a')}
    del _L0_gnn_all

    def _L1_gnn_setup():
        import jax, jax.numpy as jnp
        import numpy as np
        ALPHA = 0.2
        NEG_FILL = -9000000000000000.0
        key = jax.random.key(seed)
        k_h, k_adj, k_W, k_a = jax.random.split(key, 4)
        N, D_IN, D_OUT = (4096, 128, 128)
        h = jax.random.normal(k_h, (N, D_IN), dtype=jnp.float32)
        adj = jax.random.randint(k_adj, (N, N), 0, 2, dtype=jnp.int32)
        W = jax.random.normal(k_W, (D_IN, D_OUT), dtype=jnp.float32) * (1.414 * np.sqrt(2.0 / (D_IN + D_OUT)))
        a = jax.random.normal(k_a, (2 * D_OUT, 1), dtype=jnp.float32) * (1.414 * np.sqrt(2.0 / (2 * D_OUT + 1)))
        return {'h': h, 'adj': adj, 'W': W, 'a': a}
    _L1_gnn_all = _L1_gnn_setup()
    _L1_gnn_in = {k: v for k, v in _L1_gnn_all.items() if k in ('W', 'a')}
    del _L1_gnn_all
    return {'x': x, 'adj': adj, 'L0_gnn_W': _L0_gnn_in['W'], 'L0_gnn_a': _L0_gnn_in['a'], 'L1_gnn_W': _L1_gnn_in['W'], 'L1_gnn_a': _L1_gnn_in['a']}

def reference(x, adj, L0_gnn_W, L0_gnn_a, L1_gnn_W, L1_gnn_a):
    import jax
    import jax.numpy as jnp

    def _L0_gnn_ref(h, adj, W, a):
        import jax, jax.numpy as jnp
        import numpy as np
        ALPHA = 0.2
        MASK_VAL = -9000000000000000.0
        Fout = W.shape[1]
        Wh = h @ W
        a1, a2 = (a[:Fout, 0], a[Fout:, 0])
        e = (Wh @ a1)[:, None] + (Wh @ a2)[None, :]
        e = jnp.where(e > 0, e, ALPHA * e)
        e = jnp.where(adj > 0, e, MASK_VAL)
        attention = jax.nn.softmax(e, axis=1)
        h_prime = attention @ Wh
        return jax.nn.elu(h_prime)

    def _L1_gnn_ref(h, adj, W, a):
        import jax, jax.numpy as jnp
        import numpy as np
        ALPHA = 0.2
        NEG_FILL = -9000000000000000.0
        d_out = W.shape[1]
        Wh = h @ W
        Wh1 = Wh @ a[:d_out]
        Wh2 = Wh @ a[d_out:]
        e = Wh1 + Wh2.T
        e = jnp.where(e > 0, e, ALPHA * e)
        scores = jnp.where(adj > 0, e, NEG_FILL)
        attention = jax.nn.softmax(scores, axis=1)
        h_prime = attention @ Wh
        return jax.nn.elu(h_prime)
    h = jnp.maximum(_layernorm(x, axis=-1), 0.0)
    x = x + _L0_gnn_ref(h, adj, L0_gnn_W, L0_gnn_a)
    h = jnp.maximum(_layernorm(x, axis=-1), 0.0)
    x = x + _L1_gnn_ref(h, adj, L1_gnn_W, L1_gnn_a)
    return x

_drawn_inputs = setup_inputs


def setup_inputs(seed=0):
    import zlib

    import numpy as np

    out = dict(_drawn_inputs(seed))
    spreads = {}
    factors = {}
    for name, (base, spread) in spreads.items():
        noise = np.random.default_rng([zlib.crc32(name.encode()), seed]).standard_normal(out[name].shape)
        drawn = base * np.exp(spread * noise) if base else spread * noise
        out[name] = jnp.asarray(drawn.astype(out[name].dtype))
    for name, factor in factors.items():
        out[name] = (out[name] * factor).astype(out[name].dtype)
    return out
```

```python
from contextlib import ExitStack

import concourse.bass as bass
from concourse import mybir

P = 128
ALPHA = 0.2
MASKED = 9.0e15
EPS = 1e-5

ALU = mybir.AluOpType
ACT = mybir.ActivationFunctionType
AX = mybir.AxisListType
F32 = mybir.dt.float32
I32 = mybir.dt.int32


def make_identity(nc, ident, zeroed, made):
    with nc.Block() as block:
        @block.gpsimd
        def _(pool):
            nc.gpsimd.memset(ident[:, :], 0.0).then_inc(zeroed, 1)
            pool.wait_ge(zeroed, 1)
            nc.gpsimd.affine_select(out=ident[:, :], in_=ident[:, :], compare_op=ALU.not_equal, fill=1.0,
                                    base=0, pattern=[[-1, P]], channel_multiplier=1).then_inc(made, 1)
            pool.wait_ge(made, 1)


def general_layer(nc, layer, x_in, adj, w_in, a_in, out, x_sb, ident, room, psum):
    n = adj.shape[0]
    tiles = n // P
    with ExitStack() as ctx:
        def sem(name):
            return ctx.enter_context(nc.semaphore(f"general{layer}_{name}"))

        at = [0]

        def take(words):
            at[0] += words
            return room[:, at[0] - words:at[0]]

        adj_tile = take(n).bitcast(I32)
        score = take(n)
        prob = take(n)
        t_rows = take(n)
        v_all = take(n).rearrange("p (t f) -> p t f", f=P)
        probT = take(n).rearrange("p (t i) -> p t i", i=P)
        w_ext = take(P + 2)
        a_rep = take(2 * P)
        products = take(2 * P)
        wa2_rep = take(P)
        s_all = take(tiles)
        norm_tile = take(P)
        hT = take(P)
        norm = score.rearrange("p (t f) -> p t f", f=P)
        squares = prob.rearrange("p (t f) -> p t f", f=P)
        out_tile = take(P)
        pos = take(P)
        neg = take(P)
        mean = take(tiles)
        var = take(tiles)
        std = take(tiles)
        rstd = take(tiles)
        tmp = take(tiles)
        row_max = take(1)
        neg_max = take(1)
        row_sum = take(1)
        recip = take(1)
        _, psH, psV, psT, psP, psO = psum[0], psum[1], psum[2], psum[3], psum[4:6], psum[6]

        loaded = sem("loaded")
        wa_steps = sem("wa_steps")
        ln = sem("ln")
        norm_ready = sem("norm_ready")
        std_ready = sem("std_ready")
        h_transposed = sem("h_transposed")
        hT_ready = sem("hT_ready")
        projected = sem("projected")
        kept = sem("kept")
        adj_loaded = sem("adj_loaded")
        sc = sem("sc")
        exp_done = sem("exp_done")
        p_transposed = sem("p_transposed")
        probT_ready = sem("probT_ready")
        product = sem("product")
        ep = sem("ep")
        elu_exp = sem("elu_exp")
        stored = sem("stored")

        SC_STEPS, EP_STEPS = 8, 6
        groups = tiles // 4

        with nc.Block() as block:
            @block.sync
            def _(sp):
                if layer == 0:
                    sp.dma_start(x_sb[:, :, :], x_in.rearrange("(t p) f -> p t f", p=P)).then_inc(loaded, 16)
                sp.dma_start(w_ext[:, 0:P], w_in).then_inc(loaded, 16)
                sp.dma_start(a_rep, a_in.rearrange("c o -> o c").broadcast_to([P, 2 * P])).then_inc(loaded, 16)
                with sp.Fori(0, tiles) as i:
                    sp.wait_ge(sc, i * SC_STEPS + 1)
                    sp.dma_start(adj_tile, adj[bass.ts(i, P), :]).then_inc(adj_loaded, 16)
                if layer == 1:
                    sp.wait_ge(ep, tiles * EP_STEPS + 1)
                    sp.dma_start(out.rearrange("(t p) f -> p t f", p=P), x_sb[:, :, :]).then_inc(stored, 16)
                    sp.wait_ge(stored, 16)

            @block.tensor
            def _(pe):
                pe.wait_ge(loaded, 48 if layer == 0 else 32)
                pe.wait_ge(wa_steps, 4)
                with pe.Fori(0, tiles) as i:
                    pe.wait_ge(norm_ready, i + 1)
                    nc.tensor.transpose(psH[:, 0:P], norm_tile, ident[:, :]).then_inc(h_transposed, 1)
                    pe.wait_ge(hT_ready, i + 1)
                    nc.tensor.matmul(psV[:, 0:P + 2], hT, w_ext, start=True, stop=True)
                    nc.tensor.matmul(psT[:, 0:P], wa2_rep, hT, start=True, stop=True).then_inc(projected, 1)
                pe.sem_inc(product, 1)
                with pe.Fori(0, tiles) as i:
                    pe.wait_ge(exp_done, i + 1)
                    for g in range(groups):
                        if g < 2:
                            pe.wait_ge(probT_ready, i * groups + 1)
                        else:
                            pe.wait_ge(probT_ready, i * groups + g)
                        for k in range(4):
                            j = 4 * g + k
                            last = nc.tensor.transpose(psP[g % 2][:, k * P:(k + 1) * P],
                                                       prob[:, j * P:(j + 1) * P], ident[:, :])
                        last.then_inc(p_transposed, 1)
                    pe.wait_ge(probT_ready, i * groups + (groups + 1))
                    pe.wait_ge(ep, i * EP_STEPS + 1)
                    for j in range(tiles):
                        last = nc.tensor.matmul(psO[:, 0:P], probT[:, j, :], v_all[:, j, :],
                                                start=(j == 0), stop=(j == tiles - 1))
                    last.then_inc(product, 1)

            @block.scalar
            def _(act):
                act.wait_ge(ln, 6)
                nc.scalar.activation(std, var, ACT.Sqrt).then_inc(std_ready, 1)
                with act.Fori(0, tiles) as i:
                    act.wait_ge(h_transposed, i + 1)
                    nc.scalar.activation(hT, psH[:, 0:P], ACT.Relu).then_inc(hT_ready, 1)
                act.sem_inc(probT_ready, 1)
                with act.Fori(0, tiles) as i:
                    act.wait_ge(sc, i * SC_STEPS + (SC_STEPS + 1))
                    nc.scalar.activation(prob, score, ACT.Exp, bias=neg_max, accum_out=row_sum).then_inc(exp_done, 1)
                    act.wait_ge(product, i + 1)
                    for g in range(groups):
                        act.wait_ge(p_transposed, i * groups + (g + 1))
                        nc.scalar.activation(probT[:, 4 * g:4 * g + 4, :], psP[g % 2][:, 0:4 * P].rearrange("p (t i) -> p t i", i=P),
                                             ACT.Copy).then_inc(probT_ready, 1)
                    act.wait_ge(ep, i * EP_STEPS + 4)
                    nc.scalar.activation(neg, neg, ACT.Exp).then_inc(elu_exp, 1)

            @block.vector
            def _(dve):
                def run(count, base, signal, ops):
                    for k, op in enumerate(ops):
                        op().then_inc(signal, 1)
                        dve.wait_ge(signal, base + (count + k + 1))

                dve.wait_ge(loaded, 48 if layer == 0 else 32)
                for c in range(2):
                    nc.vector.tensor_tensor(products[:, c * P:(c + 1) * P], w_ext[:, 0:P], a_rep[:, c * P:(c + 1) * P],
                                            ALU.mult).then_inc(wa_steps, 1)
                dve.wait_ge(wa_steps, 2)
                nc.vector.reduce_sum(w_ext[:, P:P + 2], products.rearrange("p (c f) -> p c f", c=2), AX.X).then_inc(wa_steps, 1)
                dve.wait_ge(wa_steps, 3)
                nc.vector.tensor_copy(wa2_rep, w_ext[:, P + 1:P + 2].broadcast_to([P, P])).then_inc(wa_steps, 1)
                per_row = lambda v: v.unsqueeze(2).broadcast_to([P, tiles, P])
                run(0, 0, ln, [
                    lambda: nc.vector.reduce_sum(mean, x_sb[:, :, :], AX.X),
                    lambda: nc.vector.tensor_scalar(mean, mean, 1.0 / P, None, ALU.mult),
                    lambda: nc.vector.tensor_tensor(norm, x_sb[:, :, :], per_row(mean), ALU.subtract),
                    lambda: nc.vector.tensor_tensor(squares, norm, norm, ALU.mult),
                    lambda: nc.vector.reduce_sum(var, squares, AX.X),
                    lambda: nc.vector.tensor_scalar(var, var, 1.0 / P, EPS, ALU.mult, ALU.add)])
                dve.wait_ge(std_ready, 1)
                run(6, 0, ln, [
                    lambda: nc.vector.reciprocal(rstd, std),
                    lambda: nc.vector.tensor_tensor(tmp, rstd, rstd, ALU.mult),
                    lambda: nc.vector.tensor_tensor(tmp, tmp, var, ALU.mult),
                    lambda: nc.vector.tensor_scalar(tmp, tmp, -0.5, 1.5, ALU.mult, ALU.add),
                    lambda: nc.vector.tensor_tensor(rstd, rstd, tmp, ALU.mult),
                    lambda: nc.vector.tensor_tensor(norm, norm, per_row(rstd), ALU.mult)])
                with dve.Fori(0, tiles) as i:
                    nc.vector.tensor_copy(norm_tile, score[:, bass.ts(i, P)]).then_inc(norm_ready, 1)
                    dve.wait_ge(projected, i + 1)
                    nc.vector.tensor_copy(v_all[:, bass.ds(i, 1), :].rearrange("p t f -> p (t f)"), psV[:, 0:P])
                    nc.vector.tensor_copy(s_all[:, bass.ds(i, 1)], psV[:, P:P + 1])
                    nc.vector.tensor_copy(t_rows[:, bass.ts(i, P)], psT[:, 0:P]).then_inc(kept, 1)
                    dve.wait_ge(kept, i + 1)
                dve.sem_inc(sc, 1)
                dve.sem_inc(ep, 1)
                with dve.Fori(0, tiles) as i:
                    base = i * SC_STEPS + 1
                    dve.wait_ge(adj_loaded, i * 16 + 16)
                    dve.wait_ge(product, i + 1)
                    run(0, base, sc, [
                        lambda: nc.vector.tensor_scalar(score, t_rows, s_all[:, bass.ds(i, 1)], None, ALU.add),
                        lambda: nc.vector.scalar_tensor_tensor(score, score, ALPHA, score, ALU.mult, ALU.max),
                        lambda: nc.vector.tensor_scalar(prob, adj_tile, 0, None, ALU.is_gt),
                        lambda: nc.vector.tensor_tensor(score, score, prob, ALU.mult),
                        lambda: nc.vector.tensor_scalar(prob, prob, 1.0, MASKED, ALU.subtract, ALU.mult),
                        lambda: nc.vector.tensor_tensor(score, score, prob, ALU.add),
                        lambda: nc.vector.reduce_max(row_max, score, AX.X),
                        lambda: nc.vector.tensor_scalar(neg_max, row_max, -1.0, None, ALU.mult)])
                    dve.wait_ge(exp_done, i + 1)
                    dve.wait_ge(product, i + 2)
                    base_e = i * EP_STEPS + 1
                    run(0, base_e, ep, [
                        lambda: nc.vector.reciprocal(recip, row_sum),
                        lambda: nc.vector.tensor_scalar(out_tile, psO[:, 0:P], recip, None, ALU.mult),
                        lambda: nc.vector.tensor_scalar(neg, out_tile, 0.0, None, ALU.min)])
                    run(3, base_e, ep, [
                        lambda: nc.vector.tensor_scalar(pos, out_tile, 0.0, -1.0, ALU.max, ALU.add)])
                    dve.wait_ge(elu_exp, i + 1)
                    x_t = x_sb[:, bass.ds(i, 1), :].rearrange("p t f -> p (t f)")
                    run(4, base_e, ep, [
                        lambda: nc.vector.tensor_tensor(pos, pos, neg, ALU.add),
                        lambda: nc.vector.tensor_tensor(x_t, x_t, pos, ALU.add)])


def build(nc, x, adj, w0, a0, w1, a1, out):
    n = adj.shape[0]
    tiles = n // P
    with ExitStack() as ctx:
        x_sb = ctx.enter_context(nc.sbuf_tensor("x_sb", [P, tiles, P], F32))
        ident = ctx.enter_context(nc.sbuf_tensor("ident", [P, P], F32))
        room = ctx.enter_context(nc.sbuf_tensor("room", [P, 7 * n + 1024], F32))
        psum = [ctx.enter_context(nc.psum_tensor(f"bank{b}", [P, 512], F32)) for b in range(8)]
        zeroed = ctx.enter_context(nc.semaphore("zeroed"))
        made = ctx.enter_context(nc.semaphore("made"))
        make_identity(nc, ident, zeroed, made)
        for layer, (w, a) in enumerate(((w0, a0), (w1, a1))):
            general_layer(nc, layer, x, adj, w, a, out, x_sb, ident, room, psum)


INPUTS = ["x", "adj", "L0_gnn_W", "L0_gnn_a", "L1_gnn_W", "L1_gnn_a"]


def kernel(**inputs):
    import numpy as np
    import concourse.bacc as bacc
    from concourse.bass_utils import run_bass_kernel_spmd

    nc = bacc.Bacc("TRN2", target_bir_lowering=False, num_devices=1)
    arrays, args = {}, []
    for name in INPUTS:
        arrays[f"in_{name}"] = np.ascontiguousarray(inputs[name])
        a = arrays[f"in_{name}"]
        args.append(nc.dram_tensor(f"in_{name}", a.shape, mybir.dt.from_np(a.dtype), kind="ExternalInput").ap())
    shape = inputs["x"].shape
    args.append(nc.dram_tensor("out_x", shape, F32, kind="ExternalOutput").ap())
    build(nc, *args)
    result = run_bass_kernel_spmd(nc, [arrays], core_ids=[0])
    return result.results[0]["out_x"]
```

```python
from contextlib import ExitStack

import concourse.bass as bass
from concourse import mybir

P = 128
ALPHA = 0.2
MASKED = 9.0e15
EPS = 1e-5

BYTES = 4
GROUP = BYTES * P
BITS = (0x08, 0x10, 0x20, 0x40)
BIT_VALUE = (2.0 ** -6, 2.0 ** -5, 2.0 ** -3, 2.0)
ALL_BITS = 0x78787878
BLOCK_TILES = 4
BLOCK = BLOCK_TILES * P

LOW_SCALE = 2048.0
T_MAX = 6.0
V_BOUND = 10.0
DEN_UNIT = 16.0
TINY = 1e-30
HUGE = 1e30

ALU = mybir.AluOpType
ACT = mybir.ActivationFunctionType
AX = mybir.AxisListType
F32 = mybir.dt.float32
F16 = mybir.dt.float16
FP8 = mybir.dt.float8e4
I32 = mybir.dt.int32
U32 = mybir.dt.uint32
U8 = mybir.dt.uint8
I8 = mybir.dt.int8


def word(bit):
    return bit * 0x01010101


class Ticks:

    def __init__(self, eng, semaphore, step):
        self.eng, self.semaphore, self.step = eng, semaphore, step
        self.value = eng.alloc_register()
        eng.reg_mov(self.value, step)

    def wait(self, value):
        if isinstance(value, int):
            return self.eng.wait_ge(self.semaphore, value)
        self.eng.wait_ge(self.semaphore, self.value)
        self.eng.reg_add(self.value, self.value, self.step)


def fast_layer(nc, layer, x_in, adj, w_in, a_in, out, mem):
    first = layer == 0
    n = adj.shape[0]
    tiles = n // P
    blocks = n // BLOCK
    groups = n // GROUP
    words = n // BYTES // P
    assert blocks == groups == words == 8
    HALF = n // 2
    W = 2 * (P + 1)
    x_sb, s_rows, bits, parts, masks = mem["x_sb"], mem["s_rows"], mem["bits"], mem["parts"], mem["masks"]
    acc, tr, pro = mem["acc"], mem["tr"], mem["pro"]
    ident, ones = mem["ident"], mem["ones"]
    small = mem["small"]
    with ExitStack() as ctx:
        def sem(name):
            return ctx.enter_context(nc.semaphore(f"layer{layer}_{name}"))

        at = [0]

        def take(w):
            at[0] += w
            return small[:, at[0] - w:at[0]]

        wa = take(2)
        mean_rep = take(P)
        h_buf, e_buf, fill = take(P), take(P), take(P)
        s_col = take(tiles)
        t_all = take(tiles)
        neg_t = take(tiles)
        gains = take(tiles)
        w4 = take(4 * tiles).rearrange("p (t k) -> p t k", k=4)
        w4k = take(4 * tiles).rearrange("p (t k) -> p t k", k=4)
        s_neg = take(tiles)
        mean = take(tiles)
        var = take(tiles)
        std = take(tiles)
        rstd = take(tiles)
        tmp = take(tiles)
        h_sum = take(blocks)
        col = take(12)
        n2, root, c_v, k_v, h_total = (col[:, k:k + 1] for k in range(5))
        den4 = take(4)
        w4r = take(4)
        den, flag, rec = take(1), take(1), take(1)
        spare = masks[1][0][:, :, :].rearrange("p q i -> p (q i)").bitcast(F32)
        spare2 = masks[1][1][:, :, :].rearrange("p q i -> p (q i)").bitcast(F32)
        norm = [spare[:, r * BLOCK:(r + 1) * BLOCK] for r in range(2)]
        hT = [spare[:, (2 + r) * BLOCK:(3 + r) * BLOCK] for r in range(2)]
        squares = spare[:, 4 * BLOCK:4 * BLOCK + 2 * P]
        stats = spare[:, 4 * BLOCK + 2 * P:4 * BLOCK + 2 * P + 6 * tiles].rearrange("p (t k) -> p t k", k=6)
        h_rep = spare[:, 5 * BLOCK:5 * BLOCK + P]
        w_sb = spare[:, 5 * BLOCK + P:5 * BLOCK + 2 * P]
        wa1_rep = spare[:, 5 * BLOCK + 2 * P:5 * BLOCK + 3 * P]
        a_rep = spare[:, 7 * BLOCK:7 * BLOCK + 2 * P]
        wx = spare[:, 7 * BLOCK + 2 * P:7 * BLOCK + 3 * P + 1]
        t_low = [spare[:, 6 * BLOCK + 32 + 4 * r:6 * BLOCK + 36 + 4 * r] for r in range(2)]
        exps = [[spare[:, 6 * BLOCK + 8 * r + 4 * k:6 * BLOCK + 8 * r + 4 * k + 4] for k in range(2)] for r in range(2)]
        SCALED = BYTES * (P + 1)
        scaled = [[spare2[:, (2 * r + k) * SCALED:(2 * r + k + 1) * SCALED].rearrange("p (b f) -> p b f", b=BYTES)
                   for k in range(2)] for r in range(2)]

        PAIR = 2 * (P + 1) + 2
        v_sb = [spare2[:, (4 + r) * SCALED:(4 + r) * SCALED + 2 * PAIR].rearrange("p (a c) -> p a c", a=2)
                for r in range(2)]

        w2_ready = sem("w2_ready")
        n2_ready = sem("n2_ready")
        ln = sem("ln")
        loaded = sem("loaded")
        x_loaded = sem("x_loaded")
        root_ready = sem("root_ready")
        std_ready = sem("std_ready")
        norm_ready = sem("norm_ready")
        h_psum = sem("h_psum")
        hT_ready = sem("hT_ready")
        projected = sem("projected")
        s_kept = sem("s_kept")
        exp_t = sem("exp_t")
        kept = sem("kept")
        v_ready = sem("v_ready")
        pos_scaled = sem("pos_scaled")
        parts_ready = sem("parts_ready")
        head = sem("head")
        row_exp = sem("row_exp")
        mean_psum = sem("mean_psum")
        ready = sem("ready")
        adj_in = [[sem(f"adj_in{r}{h}") for h in range(2)] for r in range(2)]
        packed = [sem("packed_even"), sem("packed_odd")]
        transposed = sem("transposed")
        combined = sem("combined")
        below = sem("below")
        signed = sem("signed")
        neg_ready = sem("neg_ready")
        masks_ready = sem("masks_ready")
        acc_done = sem("acc_done")
        den_steps = sem("den_steps")
        fill_ready = sem("fill_ready")
        h_steps = sem("h_steps")
        h_ready = sem("h_ready")
        e_neg = sem("e_neg")
        e_ready = sem("e_ready")
        up_ready = sem("up_ready")
        x_done = sem("x_done")
        stored = sem("stored")

        def stages(eng, stage):
            if first:
                stage(-2, 0, True, False, False)
            stage(-1, 1, first, True, False)
            with eng.Fori(0, blocks // 2 - 1) as i:
                for r in range(2):
                    stage(i * 2 + r, r, first, True, True)
            stage(blocks - 2, 0, False, True, True)
            stage(blocks - 1, 1, False, False, True)

        with nc.Block() as block:
            @block.sync
            def _(sp):
                sp.dma_start(w_sb, w_in).then_inc(loaded, 16)
                sp.dma_start(a_rep, a_in.rearrange("c o -> o c").broadcast_to([P, 2 * P])).then_inc(loaded, 16)
                if first:
                    sp.dma_start(x_sb[:, :, :], x_in.rearrange("(t p) f -> p t f", p=P)).then_inc(x_loaded, 16)

                    def load(tile, r, h):
                        sp.dma_start(mem["adj_sb"][r][h][:, :],
                                     adj[bass.ds(tile * P, P), h * HALF:(h + 1) * HALF]).then_inc(adj_in[r][h], 16)

                    for r in range(2):
                        for h in range(2):
                            load(r, r, h)
                    with sp.Fori(0, tiles // 2 - 1) as i:
                        for r in range(2):
                            for h in range(2):
                                sp.wait_ge(packed[r], i * 2 + (h + 1))
                                load(i * 2 + (2 + r), r, h)
                else:
                    with sp.Fori(0, blocks) as b:
                        sp.wait_ge(x_done, b * BLOCK_TILES + BLOCK_TILES)
                        sp.dma_start(out[bass.ds(b * BLOCK, BLOCK), :].rearrange("(t p) f -> p t f", p=P),
                                     x_sb[:, bass.ds(b * BLOCK_TILES, BLOCK_TILES), :]).then_inc(stored, 16)
                    sp.wait_ge(stored, 16 * blocks)

            @block.gpsimd
            def _(pool):
                if first:
                    arrived = [Ticks(pool, adj_in[0][h], 16) for h in range(2)]
                    with pool.Fori(0, tiles // 2) as i:
                        pool.wait_ge(transposed, i * 2 + 1)
                        for h in range(2):
                            arrived[h].wait(i * 16 + 16)
                            nc.gpsimd.tensor_scalar(mem["bytes"][0][:, h * HALF // 4:(h + 1) * HALF // 4].bitcast(U8),
                                                    mem["adj_sb"][0][h][:, :], 0, 120.0, ALU.is_le, ALU.mult)\
                                .then_inc(packed[0], 1)

            @block.tensor
            def _(pe):
                pe.wait_ge(w2_ready, 1)
                nc.tensor.matmul(pro[:, 0, 0:P], ones[:, :], squares[:, 0:P], start=True, stop=True).then_inc(n2_ready, 1)
                pe.wait_ge(w2_ready, 7)
                pe.sem_inc(projected, 1)
                pe.sem_inc(h_psum, 1)
                with pe.Fori(0, blocks // 2) as i:
                    for r in range(2):
                        c = i * 2 + r
                        pe.wait_ge(norm_ready, c + 1)
                        pe.wait_ge(hT_ready, c + 1)
                        for k in range(BLOCK_TILES):
                            last = nc.tensor.transpose(pro[:, 0, k * P:(k + 1) * P], norm[r][:, k * P:(k + 1) * P],
                                                       ident[:, :])
                        last.then_inc(h_psum, 1)
                        pe.wait_ge(hT_ready, c + 2)
                        pe.wait_ge(s_kept, c + 1)
                        nc.tensor.matmul(pro[:, 1, :], wa1_rep, hT[r], start=True, stop=True)
                        pe.wait_ge(v_ready, c + 1)
                        for b in range(BYTES):
                            o = (b % 2) * (P + 1)
                            nc.tensor.matmul(acc[:, r, b // 2, o:o + P + 1], hT[r][:, b::BYTES], wx, start=True, stop=True)
                        for k in range(BLOCK_TILES):
                            last = nc.tensor.matmul(acc[:, r, k // 2, W + k % 2:W + k % 2 + 1], hT[r][:, k * P:(k + 1) * P],
                                                    wa[:, 0:1], start=True, stop=True)
                        last.then_inc(projected, 1)
                pe.wait_ge(head, 2)
                nc.tensor.matmul(pro[:, 0, 0:P], h_rep, w_sb, start=True, stop=True).then_inc(mean_psum, 1)

                if first:
                    pe.sem_inc(transposed, 2)
                bytes_of = mem["bytes"]
                masks_built = Ticks(pe, masks_ready, 1)
                sums_read = Ticks(pe, h_ready, 1)
                pe.wait_ge(ready, 1)

                def stage(b, r, transposing, building, multiplying):
                    for k in range(BLOCK_TILES):
                        if transposing:
                            tile = b * BLOCK_TILES + (2 * BLOCK_TILES + k)
                            pe.wait_ge(packed[k % 2], b * BLOCK_TILES + (2 * BLOCK_TILES + 2 * (k // 2) + 2))
                            pe.wait_ge(combined, tile * 4 + 1)
                            for w in range(words):
                                last = nc.tensor.transpose(tr[:, w, :], bytes_of[k % 2][:, w * P:(w + 1) * P], ident[:, :])
                            last.then_inc(transposed, 1)
                        if multiplying:
                            sums_read.wait(b * BLOCK_TILES + (k + 1))
                            for g in range(groups):
                                if k == 0:
                                    masks_built.wait(b * groups + (g + 1))
                                for byte in range(BYTES):
                                    j = BYTES * g + byte
                                    for sign in range(2):
                                        mask = masks[r][sign][:, g, k * P:(k + 1) * P].bitcast(FP8)\
                                            .rearrange("p (i b) -> p b i", b=BYTES)[:, byte, :]
                                        last = nc.tensor.matmul(acc[:, k % 2, sign, 0:W], mask, parts[:, j, sign, :],
                                                                start=(j == 0), stop=(j == tiles - 1))
                            last.then_inc(acc_done, 1)

                stages(pe, stage)

            @block.scalar
            def _(act):
                def weight_norm():
                    act.wait_ge(w2_ready, 3)
                    nc.scalar.activation(root, n2, ACT.Sqrt).then_inc(root_ready, 1)

                if first:
                    weight_norm()
                act.wait_ge(ln, 8)
                nc.scalar.activation(std, var, ACT.Sqrt).then_inc(std_ready, 1)
                if not first:
                    weight_norm()
                act.sem_inc(hT_ready, 1)
                act.sem_inc(s_kept, 1)
                act.sem_inc(v_ready, 2)

                def byte_half(h):
                    nc.scalar.activation(mem["bytes"][1][:, h * HALF // 4:(h + 1) * HALF // 4].bitcast(U8),
                                         mem["adj_sb"][1][h][:, :], ACT.Relu, bias=127.0, scale=-127.0)\
                        .then_inc(packed[1], 1)

                with act.Fori(0, blocks // 2) as i:
                    for r in range(2):
                        c = i * 2 + r
                        act.wait_ge(h_psum, c + 2)
                        act.wait_ge(root_ready, 1)
                        nc.scalar.activation(hT[r], pro[:, 0, :], ACT.Relu, accum_out=h_sum[:, bass.ds(c, 1)])\
                            .then_inc(hT_ready, 1)
                        act.wait_ge(projected, c + 2)
                        act.wait_ge(root_ready, 1)
                        nc.scalar.activation(v_sb[r], acc[:, r, :, 0:PAIR], ACT.Copy).then_inc(v_ready, 1)
                        act.wait_ge(kept, c * 4 + 1)
                        for k, slope in enumerate((1.0, ALPHA)):
                            nc.scalar.activation(exps[r][k], t_low[r], ACT.Exp, scale=slope)\
                                .then_inc(exp_t, 1)
                        nc.scalar.activation(s_rows[:, bass.ds(c * BLOCK, BLOCK)], pro[:, 1, :], ACT.Copy).then_inc(s_kept, 1)
                        act.wait_ge(kept, c * 4 + 3)
                        for b in range(BYTES):
                            o = (b % 2) * (P + 1)
                            last = nc.scalar.activation(scaled[r][0][:, b, 0:P], v_sb[r][:, b // 2, o:o + P], ACT.Copy,
                                                        scale=exps[r][0][:, b:b + 1])
                        last.then_inc(pos_scaled, 1)
                act.wait_ge(head, 3)
                nc.scalar.activation(w4[:, :, 0], s_neg, ACT.Exp).then_inc(row_exp, 1)
                act.wait_ge(head, 4)
                nc.scalar.activation(w4[:, :, 2], tmp, ACT.Exp).then_inc(row_exp, 1)
                act.wait_ge(ready, 1)

                def stage(b, r, transposing, building, multiplying):
                    nxt = b * groups + groups
                    for k in range(BLOCK_TILES):
                        if building:
                            for g in (2 * k, 2 * k + 1):
                                below_t = masks[1 - r][1][:, g, :].bitcast(I8).rearrange("p (i b) -> p b i", b=BYTES)
                                for byte in (2, 3):
                                    j = BYTES * g + byte
                                    nc.scalar.activation(below_t[:, byte, :], s_rows[:, bass.ds(b * BLOCK + BLOCK, BLOCK)],
                                                         ACT.Sign, bias=t_all[:, j:j + 1]).then_inc(signed, 1)
                        if transposing and k % 2 == 0:
                            m = b * 2 + (4 + k // 2)
                            act.wait_ge(transposed, m * 2 + 2)
                            for h in range(2):
                                act.wait_ge(adj_in[1][h], m * 16 + 16)
                                byte_half(h)
                        if multiplying:
                            tile = b * BLOCK_TILES + k
                            act.wait_ge(den_steps, tile * 6 + 3)
                            nc.scalar.activation(fill, mean_rep, ACT.Copy, scale=flag).then_inc(fill_ready, 1)
                            act.wait_ge(h_ready, tile + 3)
                            nc.scalar.activation(e_buf, h_buf, ACT.Relu, scale=-1.0).then_inc(e_neg, 1)
                            act.wait_ge(e_neg, tile + 1)
                            nc.scalar.activation(e_buf, e_buf, ACT.Exp, scale=-1.0).then_inc(e_ready, 1)
                        if building or multiplying:
                            act.wait_ge(ready, 1)

                stages(act, stage)

            @block.vector
            def _(dve):
                def weights():
                    dve.wait_ge(loaded, 32)
                    nc.vector.tensor_tensor(squares[:, 0:P], w_sb, w_sb, ALU.mult).then_inc(w2_ready, 1)
                    dve.wait_ge(n2_ready, 1)
                    nc.vector.reduce_max(n2, pro[:, 0, 0:P], AX.X).then_inc(w2_ready, 1)
                    dve.wait_ge(w2_ready, 2)
                    nc.vector.tensor_scalar(mem["bad"][:, 2 * layer:2 * layer + 1], n2, HUGE, None, ALU.is_le)
                    nc.vector.tensor_scalar(n2, n2, TINY, None, ALU.max).then_inc(w2_ready, 1)
                    products = squares.rearrange("p (c f) -> p c f", c=2)
                    nc.vector.tensor_tensor(products, a_rep.rearrange("p (c f) -> p c f", c=2),
                                            w_sb.unsqueeze(1).broadcast_to([P, 2, P]), ALU.mult).then_inc(w2_ready, 1)
                    dve.wait_ge(w2_ready, 4)
                    nc.vector.reduce_sum(wa, products, AX.X).then_inc(w2_ready, 1)
                    for g in range(groups):
                        nc.vector.memset(gains[:, BYTES * g:BYTES * (g + 1)], LOW_SCALE * BIT_VALUE[0] / BIT_VALUE[g % 4])
                    dve.wait_ge(root_ready, 1)
                    nc.vector.reciprocal(c_v, root).then_inc(w2_ready, 1)
                    nc.vector.tensor_scalar(k_v, root, DEN_UNIT / V_BOUND, None, ALU.mult)
                    dve.wait_ge(w2_ready, 6)
                    nc.vector.tensor_scalar(wx[:, 0:P], w_sb, c_v, V_BOUND, ALU.mult, ALU.mult)
                    nc.vector.tensor_copy(wx[:, P:P + 1], wa[:, 1:2])
                    nc.vector.tensor_copy(wa1_rep, wa[:, 0:1].broadcast_to([P, P])).then_inc(w2_ready, 1)

                def layer_norm():
                    if first:
                        dve.wait_ge(x_loaded, 16)
                    for t in range(tiles):
                        last = nc.vector.bn_stats(stats[:, t, :], x_sb[:, t, :])
                    last.then_inc(ln, 1)
                    me, m2e, mo, m2o = stats[:, :, 1], stats[:, :, 2], stats[:, :, 4], stats[:, :, 5]
                    dve.wait_ge(ln, 1)
                    nc.vector.tensor_tensor(mean, me, mo, ALU.add).then_inc(ln, 1)
                    nc.vector.tensor_tensor(tmp, me, mo, ALU.subtract).then_inc(ln, 1)
                    nc.vector.tensor_tensor(var, m2e, m2o, ALU.add).then_inc(ln, 1)
                    dve.wait_ge(ln, 4)
                    nc.vector.tensor_scalar(mean, mean, 0.5, None, ALU.mult).then_inc(ln, 1)
                    nc.vector.tensor_tensor(tmp, tmp, tmp, ALU.mult).then_inc(ln, 1)
                    dve.wait_ge(ln, 6)
                    nc.vector.scalar_tensor_tensor(var, tmp, P / 4.0, var, ALU.mult, ALU.add).then_inc(ln, 1)
                    dve.wait_ge(ln, 7)
                    nc.vector.tensor_scalar(var, var, 1.0 / P, EPS, ALU.mult, ALU.add).then_inc(ln, 1)
                    dve.wait_ge(std_ready, 1)
                    nc.vector.reciprocal(rstd, std).then_inc(ln, 1)
                    dve.wait_ge(ln, 9)
                    nc.vector.tensor_tensor(tmp, rstd, rstd, ALU.mult).then_inc(ln, 1)
                    dve.wait_ge(ln, 10)
                    nc.vector.tensor_tensor(tmp, tmp, var, ALU.mult).then_inc(ln, 1)
                    dve.wait_ge(ln, 11)
                    nc.vector.tensor_scalar(tmp, tmp, -0.5, 1.5, ALU.mult, ALU.add).then_inc(ln, 1)
                    dve.wait_ge(ln, 12)
                    nc.vector.tensor_tensor(rstd, rstd, tmp, ALU.mult).then_inc(ln, 1)
                    dve.wait_ge(ln, 13)

                for step in (weights, layer_norm) if first else (layer_norm, weights):
                    step()

                def prologue(c, r):
                    for k in range(BLOCK_TILES):
                        t = c * BLOCK_TILES + k
                        last = nc.vector.tensor_scalar(norm[r][:, k * P:(k + 1) * P],
                                                       x_sb[:, bass.ds(t, 1), :].rearrange("p t f -> p (t f)"),
                                                       mean[:, bass.ds(t, 1)], rstd[:, bass.ds(t, 1)],
                                                       ALU.subtract, ALU.mult)
                    last.then_inc(norm_ready, 1)
                    j = c * BYTES
                    dve.wait_ge(v_ready, c + 3)
                    t_of = v_sb[r][:, :, P:2 * (P + 1):P + 1]
                    nc.vector.tensor_scalar(t_low[r].rearrange("p (a b) -> p a b", a=2), t_of, T_MAX, -T_MAX,
                                            ALU.min, ALU.max).then_inc(kept, 1)
                    nc.vector.tensor_copy(s_col[:, bass.ds(c * BLOCK_TILES, BLOCK_TILES)].rearrange("p (a b) -> p a b", a=2),
                                          v_sb[r][:, :, W:W + 2])
                    nc.vector.tensor_copy(t_all[:, bass.ds(j, BYTES)].rearrange("p (a b) -> p a b", a=2), t_of)
                    nc.vector.tensor_scalar(neg_t[:, bass.ds(j, BYTES)].rearrange("p (a b) -> p a b", a=2), t_of,
                                            -1.0, None, ALU.mult)
                    for k in range(2):
                        dve.wait_ge(exp_t, c * 2 + (k + 1))
                        nc.vector.tensor_tensor(exps[r][k], exps[r][k], gains[:, bass.ds(j, BYTES)], ALU.mult)\
                            .then_inc(kept, 1)
                    dve.wait_ge(kept, c * 4 + 3)
                    v_of = v_sb[r][:, :, 0:2 * (P + 1)].rearrange("p a (b f) -> p a b f", b=2)[:, :, :, 0:P]
                    nc.vector.tensor_tensor(scaled[r][1][:, :, 0:P].rearrange("p (a b) f -> p a b f", a=2), v_of,
                                            exps[r][1].rearrange("p (a b) -> p a b", a=2).unsqueeze(3)
                                            .broadcast_to([P, 2, 2, P]), ALU.mult).then_inc(kept, 1)
                    for k in range(2):
                        nc.vector.tensor_scalar(scaled[r][k][:, :, P], exps[r][k], DEN_UNIT, None, ALU.mult)\
                            .then_inc(parts_ready, 1)
                    for k in (1, 0):
                        hi = parts[:, bass.ds(j, BYTES), k, 0:P + 1]
                        low = parts[:, bass.ds(j, BYTES), k, P + 1:W]
                        if k == 1:
                            dve.wait_ge(kept, c * 4 + 4)
                        else:
                            dve.wait_ge(pos_scaled, c + 1)
                        dve.wait_ge(parts_ready, c * 6 + (2 if k == 1 else 4))
                        nc.vector.tensor_scalar(hi, scaled[r][k], 1.0 / LOW_SCALE, None, ALU.mult).then_inc(parts_ready, 1)
                        dve.wait_ge(parts_ready, c * 6 + (3 if k == 1 else 5))
                        nc.vector.scalar_tensor_tensor(low, hi, -LOW_SCALE, scaled[r][k], ALU.mult, ALU.add)\
                            .then_inc(parts_ready, 1)

                with dve.Fori(0, blocks // 2) as i:
                    for r in range(2):
                        prologue(i * 2 + r, r)

                dve.wait_ge(hT_ready, blocks + 1)
                nc.vector.reduce_sum(h_total, h_sum, AX.X).then_inc(head, 1)
                dve.wait_ge(head, 1)
                nc.vector.tensor_scalar(h_rep, h_total.broadcast_to([P, P]), 1.0 / n, None, ALU.mult).then_inc(head, 1)
                dve.wait_ge(parts_ready, 6 * blocks)
                nc.vector.tensor_scalar(s_neg, s_col, 1.0 - ALPHA, 0.0, ALU.mult, ALU.min).then_inc(head, 1)
                nc.vector.tensor_scalar(tmp, s_col, ALPHA - 1.0, 0.0, ALU.mult, ALU.min).then_inc(head, 1)
                nc.vector.scalar_tensor_tensor(mean, t_all, -1.0, t_all, ALU.mult, ALU.max).then_inc(head, 1)
                dve.wait_ge(head, 5)
                nc.vector.tensor_scalar(mean, mean, T_MAX, None, ALU.is_le).then_inc(head, 1)
                dve.wait_ge(head, 6)
                nc.vector.tensor_reduce(mem["bad"][:, 2 * layer + 1:2 * layer + 2], mean, axis=AX.X, op=ALU.min)\
                    .then_inc(head, 1)
                dve.wait_ge(mean_psum, 1)
                nc.vector.tensor_copy(mean_rep, pro[:, 0, 0:P])
                dve.wait_ge(row_exp, 2)
                nc.vector.tensor_scalar(w4[:, :, 1], w4[:, :, 0], 1.0 / LOW_SCALE, None, ALU.mult).then_inc(head, 1)
                nc.vector.tensor_scalar(w4[:, :, 3], w4[:, :, 2], 1.0 / LOW_SCALE, None, ALU.mult).then_inc(head, 1)
                dve.wait_ge(head, 9)
                nc.vector.tensor_scalar(w4k, w4, k_v, None, ALU.mult).then_inc(ready, 1)

                if first:
                    dve.sem_inc(combined, 1)
                dve.sem_inc(h_ready, 2)

                def stage(b, r, transposing, building, multiplying):
                    nxt = b * groups + groups
                    row = b * BLOCK + BLOCK

                    def combine(k, step):
                        tile = b * BLOCK_TILES + (2 * BLOCK_TILES + k)
                        where = bits[:, :, bass.ds(tile * P, P)]
                        came = tr[:, step::4, :].bitcast(U32)
                        if step == 0:
                            dve.wait_ge(transposed, tile + 3)
                            nc.vector.tensor_scalar(where, came, word(BITS[0]), ALL_BITS, ALU.bitwise_and, ALU.bitwise_xor)\
                                .then_inc(combined, 1)
                        else:
                            dve.wait_ge(combined, tile * 4 + (step + 1))
                            nc.vector.scalar_tensor_tensor(where, came, word(BITS[step]), where, ALU.bitwise_and,
                                                           ALU.bitwise_xor).then_inc(combined, 1)

                    def compare(g):
                        below_t = masks[1 - r][1][:, g, :].bitcast(U8).rearrange("p (i b) -> p b i", b=BYTES)
                        for byte in (0, 1):
                            j = BYTES * g + byte
                            nc.vector.tensor_scalar(below_t[:, byte, :], s_rows[:, bass.ds(row, BLOCK)], neg_t[:, j:j + 1],
                                                    float(BITS[g % 4]), ALU.is_lt, ALU.mult).then_inc(below, 1)

                    def cut_neg(g):
                        neg = masks[1 - r][1][:, g, :]
                        dve.wait_ge(below, nxt * 2 + (2 * g + 2))
                        dve.wait_ge(signed, nxt * 2 + (2 * g + 2))
                        nc.vector.scalar_tensor_tensor(neg, neg, word(BITS[g % 4]), bits[:, g // 4, bass.ds(row, BLOCK)],
                                                       ALU.bitwise_and, ALU.bitwise_and).then_inc(neg_ready, 1)

                    def cut_pos(g):
                        dve.wait_ge(neg_ready, nxt + (g + 1))
                        nc.vector.scalar_tensor_tensor(masks[1 - r][0][:, g, :], bits[:, g // 4, bass.ds(row, BLOCK)],
                                                       word(BITS[g % 4]), masks[1 - r][1][:, g, :],
                                                       ALU.bitwise_and, ALU.bitwise_xor).then_inc(masks_ready, 1)

                    def average(k):
                        tile = b * BLOCK_TILES + k
                        sums = acc[:, k % 2, :, :]
                        w_t = w4[:, bass.ds(tile, 1), :].rearrange("p t (a b) -> p (t a) b", a=2)
                        wk_t = w4k[:, bass.ds(tile, 1), :].rearrange("p t k -> p (t k)")
                        base = tile * 6
                        dve.wait_ge(acc_done, tile + 1)
                        nc.vector.tensor_tensor(den4.rearrange("p (a b) -> p a b", a=2), sums[:, :, P:W:P + 1], w_t, ALU.mult)\
                            .then_inc(den_steps, 1)
                        if building:
                            cut_pos(2 * k + 1)
                        dve.wait_ge(den_steps, base + 1)
                        nc.vector.reduce_sum(den, den4, AX.X).then_inc(den_steps, 1)
                        dve.wait_ge(den_steps, base + 2)
                        nc.vector.tensor_scalar(flag, den, 0.0, None, ALU.is_equal).then_inc(den_steps, 1)
                        nc.vector.tensor_scalar(den, den, TINY, None, ALU.max).then_inc(den_steps, 1)
                        dve.wait_ge(den_steps, base + 4)
                        nc.vector.reciprocal(rec, den).then_inc(den_steps, 1)
                        dve.wait_ge(den_steps, base + 5)
                        nc.vector.tensor_scalar(w4r, wk_t, rec, None, ALU.mult).then_inc(den_steps, 1)
                        dve.wait_ge(den_steps, base + 6)
                        dve.wait_ge(fill_ready, tile + 1)
                        before = fill
                        for m in range(4):
                            o = (m % 2) * (P + 1)
                            if m:
                                dve.wait_ge(h_steps, tile * 3 + m)
                            nc.vector.scalar_tensor_tensor(h_buf, sums[:, m // 2, o:o + P], w4r[:, m:m + 1], before,
                                                           ALU.mult, ALU.add).then_inc(h_steps if m < 3 else h_ready, 1)
                            before = h_buf

                    def update(k):
                        tile = b * BLOCK_TILES + k
                        x_t = x_sb[:, bass.ds(tile, 1), :].rearrange("p t f -> p (t f)")
                        dve.wait_ge(e_ready, tile + 1)
                        nc.vector.scalar_tensor_tensor(e_buf, e_buf, -1.0, h_buf, ALU.add, ALU.max).then_inc(up_ready, 1)
                        dve.wait_ge(up_ready, tile + 1)
                        nc.vector.tensor_tensor(x_t, x_t, e_buf, ALU.add).then_inc(x_done, 1)

                    for k in range(BLOCK_TILES):
                        if transposing:
                            combine(k, 0)
                        if multiplying and k:
                            update(k - 1)
                        if building:
                            compare(2 * k)
                        if transposing:
                            combine(k, 1)
                        if building:
                            cut_neg(2 * k)
                        if transposing:
                            combine(k, 2)
                        if building:
                            compare(2 * k + 1)
                            cut_pos(2 * k)
                        if transposing:
                            combine(k, 3)
                        if building:
                            cut_neg(2 * k + 1)
                        if multiplying:
                            average(k)
                        elif building:
                            cut_pos(2 * k + 1)
                    if multiplying:
                        update(BLOCK_TILES - 1)

                stages(dve, stage)


def general_layer(nc, layer, x_in, adj, w_in, a_in, out, x_sb, ident, room, psum):
    n = adj.shape[0]
    tiles = n // P
    with ExitStack() as ctx:
        def sem(name):
            return ctx.enter_context(nc.semaphore(f"general{layer}_{name}"))

        at = [0, 0]

        def take(words, part=1):
            at[part] += words
            return room[part][:, at[part] - words:at[part]]

        adj_tile = take(n, 0).bitcast(I32)
        score = take(n, 0)
        prob = take(n, 0)
        t_rows = take(n, 0)
        v_all = take(n, 0).rearrange("p (t f) -> p t f", f=P)
        probT = take(n, 0).rearrange("p (t i) -> p t i", i=P)
        w_ext = take(P + 2)
        a_rep = take(2 * P)
        products = take(2 * P)
        wa2_rep = take(P)
        s_all = take(tiles)
        norm_tile = take(P)
        hT = take(P)
        norm = score.rearrange("p (t f) -> p t f", f=P)
        squares = prob.rearrange("p (t f) -> p t f", f=P)
        out_tile = take(P)
        pos = take(P)
        neg = take(P)
        mean = take(tiles)
        var = take(tiles)
        std = take(tiles)
        rstd = take(tiles)
        tmp = take(tiles)
        row_max = take(1)
        neg_max = take(1)
        row_sum = take(1)
        recip = take(1)
        _, psH, psV, psT, psP, psO = psum[0], psum[1], psum[2], psum[3], psum[4:6], psum[6]

        loaded = sem("loaded")
        wa_steps = sem("wa_steps")
        ln = sem("ln")
        norm_ready = sem("norm_ready")
        std_ready = sem("std_ready")
        h_transposed = sem("h_transposed")
        hT_ready = sem("hT_ready")
        projected = sem("projected")
        kept = sem("kept")
        adj_loaded = sem("adj_loaded")
        sc = sem("sc")
        exp_done = sem("exp_done")
        p_transposed = sem("p_transposed")
        probT_ready = sem("probT_ready")
        product = sem("product")
        ep = sem("ep")
        elu_exp = sem("elu_exp")
        stored = sem("stored")

        SC_STEPS, EP_STEPS = 8, 6
        groups = tiles // 4

        with nc.Block() as block:
            @block.gpsimd
            def _(pool):
                if layer == 0:
                    pool.dma_start(x_sb[:, :, :], x_in.rearrange("(t p) f -> p t f", p=P)).then_inc(loaded, 16)
                pool.dma_start(w_ext[:, 0:P], w_in).then_inc(loaded, 16)
                pool.dma_start(a_rep, a_in.rearrange("c o -> o c").broadcast_to([P, 2 * P])).then_inc(loaded, 16)

            @block.sync
            def _(sp):
                with sp.Fori(0, tiles) as i:
                    sp.wait_ge(sc, i * SC_STEPS + 1)
                    sp.dma_start(adj_tile, adj[bass.ts(i, P), :]).then_inc(adj_loaded, 16)
                if layer == 1:
                    sp.wait_ge(ep, tiles * EP_STEPS + 1)
                    sp.dma_start(out.rearrange("(t p) f -> p t f", p=P), x_sb[:, :, :]).then_inc(stored, 16)
                    sp.wait_ge(stored, 16)

            @block.tensor
            def _(pe):
                pe.wait_ge(loaded, 48 if layer == 0 else 32)
                pe.wait_ge(wa_steps, 4)
                with pe.Fori(0, tiles) as i:
                    pe.wait_ge(norm_ready, i + 1)
                    nc.tensor.transpose(psH[:, 0:P], norm_tile, ident[:, :]).then_inc(h_transposed, 1)
                    pe.wait_ge(hT_ready, i + 1)
                    nc.tensor.matmul(psV[:, 0:P + 2], hT, w_ext, start=True, stop=True)
                    nc.tensor.matmul(psT[:, 0:P], wa2_rep, hT, start=True, stop=True).then_inc(projected, 1)
                pe.sem_inc(product, 1)
                with pe.Fori(0, tiles) as i:
                    pe.wait_ge(exp_done, i + 1)
                    for g in range(groups):
                        if g < 2:
                            pe.wait_ge(probT_ready, i * groups + 1)
                        else:
                            pe.wait_ge(probT_ready, i * groups + g)
                        for k in range(4):
                            j = 4 * g + k
                            last = nc.tensor.transpose(psP[g % 2][:, k * P:(k + 1) * P],
                                                       prob[:, j * P:(j + 1) * P], ident[:, :])
                        last.then_inc(p_transposed, 1)
                    pe.wait_ge(probT_ready, i * groups + (groups + 1))
                    pe.wait_ge(ep, i * EP_STEPS + 1)
                    for j in range(tiles):
                        last = nc.tensor.matmul(psO[:, 0:P], probT[:, j, :], v_all[:, j, :],
                                                start=(j == 0), stop=(j == tiles - 1))
                    last.then_inc(product, 1)

            @block.scalar
            def _(act):
                act.wait_ge(ln, 6)
                nc.scalar.activation(std, var, ACT.Sqrt).then_inc(std_ready, 1)
                with act.Fori(0, tiles) as i:
                    act.wait_ge(h_transposed, i + 1)
                    nc.scalar.activation(hT, psH[:, 0:P], ACT.Relu).then_inc(hT_ready, 1)
                act.sem_inc(probT_ready, 1)
                with act.Fori(0, tiles) as i:
                    act.wait_ge(sc, i * SC_STEPS + (SC_STEPS + 1))
                    nc.scalar.activation(prob, score, ACT.Exp, bias=neg_max, accum_out=row_sum).then_inc(exp_done, 1)
                    act.wait_ge(product, i + 1)
                    for g in range(groups):
                        act.wait_ge(p_transposed, i * groups + (g + 1))
                        nc.scalar.activation(probT[:, 4 * g:4 * g + 4, :], psP[g % 2][:, 0:4 * P].rearrange("p (t i) -> p t i", i=P),
                                             ACT.Copy).then_inc(probT_ready, 1)
                    act.wait_ge(ep, i * EP_STEPS + 4)
                    nc.scalar.activation(neg, neg, ACT.Exp).then_inc(elu_exp, 1)

            @block.vector
            def _(dve):
                def run(count, base, signal, ops):
                    for k, op in enumerate(ops):
                        op().then_inc(signal, 1)
                        dve.wait_ge(signal, base + (count + k + 1))

                dve.wait_ge(loaded, 48 if layer == 0 else 32)
                for c in range(2):
                    nc.vector.tensor_tensor(products[:, c * P:(c + 1) * P], w_ext[:, 0:P], a_rep[:, c * P:(c + 1) * P],
                                            ALU.mult).then_inc(wa_steps, 1)
                dve.wait_ge(wa_steps, 2)
                nc.vector.reduce_sum(w_ext[:, P:P + 2], products.rearrange("p (c f) -> p c f", c=2), AX.X).then_inc(wa_steps, 1)
                dve.wait_ge(wa_steps, 3)
                nc.vector.tensor_copy(wa2_rep, w_ext[:, P + 1:P + 2].broadcast_to([P, P])).then_inc(wa_steps, 1)
                per_row = lambda v: v.unsqueeze(2).broadcast_to([P, tiles, P])
                run(0, 0, ln, [
                    lambda: nc.vector.reduce_sum(mean, x_sb[:, :, :], AX.X),
                    lambda: nc.vector.tensor_scalar(mean, mean, 1.0 / P, None, ALU.mult),
                    lambda: nc.vector.tensor_tensor(norm, x_sb[:, :, :], per_row(mean), ALU.subtract),
                    lambda: nc.vector.tensor_tensor(squares, norm, norm, ALU.mult),
                    lambda: nc.vector.reduce_sum(var, squares, AX.X),
                    lambda: nc.vector.tensor_scalar(var, var, 1.0 / P, EPS, ALU.mult, ALU.add)])
                dve.wait_ge(std_ready, 1)
                run(6, 0, ln, [
                    lambda: nc.vector.reciprocal(rstd, std),
                    lambda: nc.vector.tensor_tensor(tmp, rstd, rstd, ALU.mult),
                    lambda: nc.vector.tensor_tensor(tmp, tmp, var, ALU.mult),
                    lambda: nc.vector.tensor_scalar(tmp, tmp, -0.5, 1.5, ALU.mult, ALU.add),
                    lambda: nc.vector.tensor_tensor(rstd, rstd, tmp, ALU.mult),
                    lambda: nc.vector.tensor_tensor(norm, norm, per_row(rstd), ALU.mult)])
                with dve.Fori(0, tiles) as i:
                    nc.vector.tensor_copy(norm_tile, score[:, bass.ts(i, P)]).then_inc(norm_ready, 1)
                    dve.wait_ge(projected, i + 1)
                    nc.vector.tensor_copy(v_all[:, bass.ds(i, 1), :].rearrange("p t f -> p (t f)"), psV[:, 0:P])
                    nc.vector.tensor_copy(s_all[:, bass.ds(i, 1)], psV[:, P:P + 1])
                    nc.vector.tensor_copy(t_rows[:, bass.ts(i, P)], psT[:, 0:P]).then_inc(kept, 1)
                    dve.wait_ge(kept, i + 1)
                dve.sem_inc(sc, 1)
                dve.sem_inc(ep, 1)
                with dve.Fori(0, tiles) as i:
                    base = i * SC_STEPS + 1
                    dve.wait_ge(adj_loaded, i * 16 + 16)
                    dve.wait_ge(product, i + 1)
                    run(0, base, sc, [
                        lambda: nc.vector.tensor_scalar(score, t_rows, s_all[:, bass.ds(i, 1)], None, ALU.add),
                        lambda: nc.vector.scalar_tensor_tensor(score, score, ALPHA, score, ALU.mult, ALU.max),
                        lambda: nc.vector.tensor_scalar(prob, adj_tile, 0, None, ALU.is_gt),
                        lambda: nc.vector.tensor_tensor(score, score, prob, ALU.mult),
                        lambda: nc.vector.tensor_scalar(prob, prob, 1.0, MASKED, ALU.subtract, ALU.mult),
                        lambda: nc.vector.tensor_tensor(score, score, prob, ALU.add),
                        lambda: nc.vector.reduce_max(row_max, score, AX.X),
                        lambda: nc.vector.tensor_scalar(neg_max, row_max, -1.0, None, ALU.mult)])
                    dve.wait_ge(exp_done, i + 1)
                    dve.wait_ge(product, i + 2)
                    base_e = i * EP_STEPS + 1
                    run(0, base_e, ep, [
                        lambda: nc.vector.reciprocal(recip, row_sum),
                        lambda: nc.vector.tensor_scalar(out_tile, psO[:, 0:P], recip, None, ALU.mult),
                        lambda: nc.vector.tensor_scalar(neg, out_tile, 0.0, None, ALU.min)])
                    run(3, base_e, ep, [
                        lambda: nc.vector.tensor_scalar(pos, out_tile, 0.0, -1.0, ALU.max, ALU.add)])
                    dve.wait_ge(elu_exp, i + 1)
                    x_t = x_sb[:, bass.ds(i, 1), :].rearrange("p t f -> p (t f)")
                    run(4, base_e, ep, [
                        lambda: nc.vector.tensor_tensor(pos, pos, neg, ALU.add),
                        lambda: nc.vector.tensor_tensor(x_t, x_t, pos, ALU.add)])


def build(nc, x, adj, w0, a0, w1, a1, out):
    n = adj.shape[0]
    tiles = n // P
    with ExitStack() as ctx:
        def sb(name, shape, dtype):
            return ctx.enter_context(nc.sbuf_tensor(name, shape, dtype))

        def sem(name):
            return ctx.enter_context(nc.semaphore(name))

        mem = {
            "x_sb": sb("x_sb", [P, tiles, P], F32),
            "s_rows": sb("s_rows", [P, n], F32),
            "bits": sb("bits", [P, 2, n], U32),
            "parts": sb("parts", [P, tiles, 2, 2 * (P + 1)], F16),
            "bytes": [sb(f"bytes{r}", [P, n // 4], F32) for r in range(2)],
            "ident": sb("ident", [P, P], F32),
            "ones": sb("ones", [P, P], F32),
            "small": sb("small", [P, 1200], F32),
            "bad": sb("bad", [P, 4], F32),
        }
        verdict = sb("verdict", [P, 2], F32)
        verdict_int = sb("verdict_int", [1, 1], I32)
        room = sb("room", [P, 2 * 2 * n + 2 * n], F32)
        masks = [[room[:, (2 * r + k) * n:(2 * r + k + 1) * n].bitcast(U32).rearrange("p (g i) -> p g i", i=BLOCK)
                  for k in range(2)] for r in range(2)]
        mem["masks"] = masks
        half = n // 2
        mem["adj_sb"] = [[room[:, 4 * n + (2 * r + h) * half:4 * n + (2 * r + h + 1) * half].bitcast(I32)
                          for h in range(2)] for r in range(2)]
        psum = ctx.enter_context(nc.psum_tensor("psum", [P, 8, 512], F32))
        mem["acc"] = psum[:, 0:4, :].rearrange("p (r s) c -> p r s c", r=2)
        mem["tr"] = psum[:, 4:6, :].rearrange("p b (w i) -> p (b w) i", i=P)
        mem["pro"] = psum[:, 6:8, :]

        zeroed, made = sem("zeroed"), sem("made")
        with nc.Block() as block:
            @block.gpsimd
            def _(pool):
                nc.gpsimd.memset(mem["ones"][:, :], 1.0).then_inc(made, 1)
                nc.gpsimd.memset(mem["ident"][:, :], 0.0).then_inc(zeroed, 1)
                pool.wait_ge(zeroed, 1)
                nc.gpsimd.affine_select(out=mem["ident"][:, :], in_=mem["ident"][:, :], compare_op=ALU.not_equal, fill=1.0,
                                        base=0, pattern=[[-1, P]], channel_multiplier=1).then_inc(made, 1)
                pool.wait_ge(made, 2)

        for layer, (w, a) in enumerate(((w0, a0), (w1, a1))):
            fast_layer(nc, layer, x, adj, w, a, out, mem)

        checks, counted, judged = sem("checks"), sem("counted"), sem("judged")
        with nc.Block() as block:
            @block.vector
            def _(dve):
                nc.vector.tensor_reduce(verdict[:, 0:1], mem["bad"][:, :], axis=AX.X, op=ALU.min).then_inc(checks, 1)
                dve.wait_ge(checks, 1)
                nc.vector.tensor_scalar(verdict[:, 1:2], verdict[:, 0:1], -1.0, 1.0, ALU.mult, ALU.add).then_inc(checks, 1)
                dve.wait_ge(counted, 1)
                nc.vector.tensor_copy(verdict_int[:, :], psum[0:1, 6, 0:1]).then_inc(judged, 1)
                dve.wait_ge(judged, 1)

            @block.tensor
            def _(pe):
                pe.wait_ge(checks, 2)
                nc.tensor.matmul(psum[0:1, 6, 0:1], verdict[:, 1:2], mem["ones"][:, 0:1], start=True, stop=True)\
                    .then_inc(counted, 1)

        failed = nc.values_load(verdict_int[0:1, 0:1], min_val=0, max_val=P)
        with nc.If(failed > 0):
            banks = [psum[:, b, :] for b in range(8)]
            general_room = [room[:, :], mem["bits"][:, :, :].rearrange("p a b -> p (a b)").bitcast(F32)]
            for layer, (w, a) in enumerate(((w0, a0), (w1, a1))):
                general_layer(nc, layer, x, adj, w, a, out, mem["x_sb"], mem["ident"], general_room, banks)


INPUTS = ["x", "adj", "L0_gnn_W", "L0_gnn_a", "L1_gnn_W", "L1_gnn_a"]


def kernel(**inputs):
    import numpy as np
    import concourse.bacc as bacc
    from concourse.bass_utils import run_bass_kernel_spmd

    nc = bacc.Bacc("TRN2", target_bir_lowering=False, num_devices=1)
    arrays, args = {}, []
    for name in INPUTS:
        arrays[f"in_{name}"] = np.ascontiguousarray(inputs[name])
        a = arrays[f"in_{name}"]
        args.append(nc.dram_tensor(f"in_{name}", a.shape, mybir.dt.from_np(a.dtype), kind="ExternalInput").ap())
    shape = inputs["x"].shape
    args.append(nc.dram_tensor("out_x", shape, F32, kind="ExternalOutput").ap())
    build(nc, *args)
    result = run_bass_kernel_spmd(nc, [arrays], core_ids=[0])
    return result.results[0]["out_x"]
```

```python
from contextlib import ExitStack

import concourse.bass as bass
from concourse import mybir

P = 128
ALPHA = 0.2
MASKED = 9.0e15
EPS = 1e-5

BYTES = 4
GROUP = BYTES * P
BITS = (0x08, 0x10, 0x20, 0x40)
BIT_VALUE = (2.0 ** -6, 2.0 ** -5, 2.0 ** -3, 2.0)
ALL_BITS = 0x78787878
BLOCK_TILES = 4
BLOCK = BLOCK_TILES * P

LOW_SCALE = 2048.0
T_MAX = 6.0
V_BOUND = 10.0
DEN_UNIT = 16.0
TINY = 1e-30
HUGE = 1e30

ALU = mybir.AluOpType
ACT = mybir.ActivationFunctionType
AX = mybir.AxisListType
F32 = mybir.dt.float32
F16 = mybir.dt.float16
FP8 = mybir.dt.float8e4
I32 = mybir.dt.int32
U32 = mybir.dt.uint32
U8 = mybir.dt.uint8
I8 = mybir.dt.int8


def word(bit):
    return bit * 0x01010101


class Ticks:

    def __init__(self, eng, semaphore, step):
        self.eng, self.semaphore, self.step = eng, semaphore, step
        self.value = eng.alloc_register()
        eng.reg_mov(self.value, step)

    def wait(self, value):
        if isinstance(value, int):
            return self.eng.wait_ge(self.semaphore, value)
        self.eng.wait_ge(self.semaphore, self.value)
        self.eng.reg_add(self.value, self.value, self.step)


def fast_layer(ctx, nc, layer, x_in, adj, w_in, a_in, out, mem, before=None):
    first = layer == 0
    n = adj.shape[0]
    tiles = n // P
    blocks = n // BLOCK
    groups = n // GROUP
    words = n // BYTES // P
    assert blocks == groups == words == 8
    HALF = n // 2
    W = 2 * (P + 1)
    x_sb, s_rows, bits, parts, masks = mem["x_sb"], mem["s_rows"], mem["bits"], mem["parts"], mem["masks"]
    acc, tr, pro = mem["acc"], mem["tr"], mem["pro"]
    ident, ones = mem["ident"], mem["ones"]
    small = mem["small"]

    def sem(name):
        return ctx.enter_context(nc.semaphore(f"layer{layer}_{name}"))

    at = [0]

    def take(w):
        at[0] += w
        return small[:, at[0] - w:at[0]]

    wa = take(2)
    mean_rep = take(P)
    h_buf, e_buf, fill = take(P), take(P), take(P)
    s_col = take(tiles)
    t_all = take(tiles)
    neg_t = take(tiles)
    gains = take(tiles)
    w4 = take(4 * tiles).rearrange("p (t k) -> p t k", k=4)
    w4k = take(4 * tiles).rearrange("p (t k) -> p t k", k=4)
    s_neg = take(tiles)
    mean = take(tiles)
    var = take(tiles)
    std = take(tiles)
    rstd = take(tiles)
    tmp = take(tiles)
    h_sum = take(blocks)
    col = take(12)
    n2, root, c_v, k_v, h_total = (col[:, k:k + 1] for k in range(5))
    den4 = take(4)
    w4r = take(4)
    den, flag, rec = take(1), take(1), take(1)
    spare = masks[1][0][:, :, :].rearrange("p q i -> p (q i)").bitcast(F32)
    spare2 = masks[1][1][:, :, :].rearrange("p q i -> p (q i)").bitcast(F32)
    regions = {"early": [mem["early"], 0], "late": [spare, 0]}

    def place(region, width):
        buf, start = regions[region]
        regions[region][1] += width
        return buf[:, start:start + width]

    w_sb = place("early", P)
    a_rep = place("early", 2 * P)
    stats = place("early", 6 * tiles).rearrange("p (t k) -> p t k", k=6)
    squares = place("early", P)
    norm = [place("late", BLOCK) for r in range(2)]
    hT = [place("late", BLOCK) for r in range(2)]
    products = place("late", 2 * P).rearrange("p (c f) -> p c f", c=2)
    h_rep = place("late", P)
    wa1_rep = place("late", P)
    wx = place("late", P + 1)
    t_low = [place("late", 4) for r in range(2)]
    exps = [place("late", 8).rearrange("p (k b) -> p k b", k=2) for r in range(2)]
    scaled = [spare2[:, r * 2 * BYTES * (P + 1):(r + 1) * 2 * BYTES * (P + 1)]
              .rearrange("p (k b f) -> p k b f", k=2, b=BYTES) for r in range(2)]
    PAIR = 2 * (P + 1) + 2
    at_v = 4 * BYTES * (P + 1)
    v_sb = [spare2[:, at_v + 2 * r * PAIR:at_v + 2 * (r + 1) * PAIR].rearrange("p (a c) -> p a c", a=2)
            for r in range(2)]

    v_psum = [acc[:, r, :, :] for r in range(2)] if first else [mem["tr_banks"]] * 2

    X_PARTS = 4
    if first:
        LN_PARTS = [range(tiles // X_PARTS), range(tiles // X_PARTS, tiles)]
    else:
        cuts = [0] + [b * BLOCK_TILES for b in (blocks - 3, blocks - 1, blocks)]
        LN_PARTS = [range(*pair) for pair in zip(cuts, cuts[1:])]
    LN_STEPS = 13
    EARLY_GROUPS = 0 if first else 3

    def early_groups(c):
        done = 2 * (c - (blocks - 3)) + 1
        return range(done, min(done + 2, EARLY_GROUPS))

    w2_ready = sem("w2_ready")
    n2_ready = sem("n2_ready")
    ln = sem("ln")
    loaded = sem("loaded")
    x_loaded = [sem(f"x_loaded{part}") for part in range(X_PARTS)]
    root_ready = sem("root_ready")
    std_ready = sem("std_ready")
    norm_ready = sem("norm_ready")
    h_psum = sem("h_psum")
    hT_ready = sem("hT_ready")
    projected = sem("projected")
    s_psum = sem("s_psum")
    s_kept = sem("s_kept")
    v_ready = sem("v_ready")
    bounded = sem("bounded")
    exp_t = sem("exp_t")
    gained = sem("gained")
    v_scaled = sem("v_scaled")
    hi_ready = sem("hi_ready")
    parts_ready = sem("parts_ready")
    head = sem("head")
    row_exp = sem("row_exp")
    mean_psum = sem("mean_psum")
    ready = sem("ready")
    adj_in = [[sem(f"adj_in_{name}{h}") for h in range(2)] for name in ("pool", "act")]
    packed = [sem("packed_pool"), sem("packed_act")]
    transposed = sem("transposed")
    combined = sem("combined")
    below = sem("below")
    signed = sem("signed")
    neg_ready = sem("neg_ready")
    masks_ready = sem("masks_ready")
    acc_done = sem("acc_done")
    den_steps = sem("den_steps")
    fill_ready = sem("fill_ready")
    h_steps = sem("h_steps")
    h_ready = sem("h_ready")
    e_neg = sem("e_neg")
    e_ready = sem("e_ready")
    up_ready = sem("up_ready")
    x_done = sem("x_done")
    stored = sem("stored")

    POOL, SCALAR = 0, 1
    POOL_TILE = 2
    ACT_TILES = (0, 1, 3)
    dve_bytes = ((0, 1), (0,)) if first else ((0,), (0,))
    act_bytes = [[byte for byte in range(BYTES) if byte not in mine] for mine in dve_bytes]

    def compared(by, b, g):
        whole, odd = g // 2, g % 2
        per_pair = len(by[0]) + len(by[1])
        return b * (groups // 2 * per_pair) + (whole * per_pair + len(by[0]) + odd * len(by[1]))

    def act_tile(b, k):
        return b * 3 + (ACT_TILES.index(k % BLOCK_TILES) + 3 * (k // BLOCK_TILES))

    def prologue_steps(eng, step):
        with eng.Fori(0, blocks // 2 - 2) as i:
            for r in range(2):
                step(i * 2 + r, i, r)
        for c in range(blocks - 4, blocks):
            step(c, c // 2, c % 2)

    def stages(eng, stage, next_layer):
        stage(-1, 1, first, first, True, False, None)
        stage(0, 0, first, first, True, True, None)
        with eng.Fori(0, blocks // 2 - 2) as i:
            stage(i * 2 + 1, 1, first, first, True, True, None)
            stage(i * 2 + 2, 0, first, first, True, True, None)
        stage(blocks - 3, 1, first, False, True, True, None)
        stage(blocks - 2, 0, False, False, True, True, next_layer)
        stage(blocks - 1, 1, False, False, False, True, next_layer)

    def sync(sp):
        if before:
            sp.wait_ge(before["transposed"], tiles + 2)
        sp.dma_start(w_sb, w_in).then_inc(loaded, 16)
        sp.dma_start(a_rep, a_in.rearrange("c o -> o c").broadcast_to([P, 2 * P])).then_inc(loaded, 16)
        if first:
            for part in range(X_PARTS):
                of_part = slice(part * tiles // X_PARTS, (part + 1) * tiles // X_PARTS)
                sp.dma_start(x_sb[:, of_part, :], x_in.rearrange("(t p) f -> p t f", p=P)[:, of_part, :])\
                    .then_inc(x_loaded[part], 16)

            def load(who, tile, h):
                sp.dma_start(mem["adj_sb"][who][h][:, :], adj[bass.ds(tile * P, P), h * HALF:(h + 1) * HALF])\
                    .then_inc(adj_in[who][h], 16)

            def load_for_act(tile, m):
                for h in range(2):
                    sp.wait_ge(packed[SCALAR], m * 2 + (h - 1))
                    load(SCALAR, tile, h)

            def load_for_pool(tile, m, h):
                sp.wait_ge(packed[POOL], m * 2 + (h - 1))
                load(POOL, tile, h)

            for who, tile in ((SCALAR, 0), (POOL, POOL_TILE)):
                for h in range(2):
                    load(who, tile, h)
            with sp.Fori(0, blocks - 1) as b:
                load_for_act(b * 4 + 1, act_tile(b, 1))
                load_for_pool(b * 4 + (4 + POOL_TILE), b + 1, 0)
                load_for_act(b * 4 + 3, act_tile(b, 3))
                load_for_pool(b * 4 + (4 + POOL_TILE), b + 1, 1)
                load_for_act(b * 4 + 4, act_tile(b, 4))
            load_for_act(tiles - 3, act_tile(blocks - 1, 1))
            load_for_act(tiles - 1, act_tile(blocks - 1, 3))
        else:
            def store(row_tile, count):
                sp.wait_ge(x_done, row_tile + count)
                sp.dma_start(out[bass.ds(row_tile * P, count * P), :].rearrange("(t p) f -> p t f", p=P),
                             x_sb[:, bass.ds(row_tile, count), :]).then_inc(stored, 16)

            with sp.Fori(0, blocks - 1) as b:
                store(b * BLOCK_TILES, BLOCK_TILES)
            for row_tile in range(tiles - BLOCK_TILES, tiles):
                store(row_tile, 1)
            sp.wait_ge(stored, 16 * (blocks - 1 + BLOCK_TILES))

    def gpsimd(pool):
        if first:
            arrived = [Ticks(pool, adj_in[POOL][h], 16) for h in range(2)]
            with pool.Fori(0, blocks) as m:
                pool.wait_ge(transposed, m * 4 + (POOL_TILE - 4 + 3))
                for h in range(2):
                    arrived[h].wait(m * 16 + 16)
                    nc.gpsimd.tensor_scalar(mem["bytes"][POOL][:, h * HALF // 4:(h + 1) * HALF // 4].bitcast(U8),
                                            mem["adj_sb"][POOL][h][:, :], 0, 120.0, ALU.is_le, ALU.mult)\
                        .then_inc(packed[POOL], 1)

    def tensor_program(pe):
        def transpose_h(c, r):
            pe.wait_ge(norm_ready, c + 1)
            for k in range(BLOCK_TILES):
                last = nc.tensor.transpose(pro[:, 0, k * P:(k + 1) * P], norm[r][:, k * P:(k + 1) * P], ident[:, :])
            last.then_inc(h_psum, 1)

        def transpose_adj(tile, who, packed_halves):
            pe.wait_ge(packed[who], packed_halves)
            pe.wait_ge(combined, tile * 4 + 1)
            for w in range(words):
                last = nc.tensor.transpose(tr[:, w, :], mem["bytes"][who][:, w * P:(w + 1) * P], ident[:, :])
            last.then_inc(transposed, 1)

        def project(c, i, r):
            pe.wait_ge(hT_ready, c + 1)
            pe.wait_ge(v_ready, c + (1 if first else 2))
            for b in range(BYTES):
                o = (b % 2) * (P + 1)
                nc.tensor.matmul(v_psum[r][:, b // 2, o:o + P + 1], hT[r][:, b::BYTES], wx, start=True, stop=True)
            for k in range(BLOCK_TILES):
                last = nc.tensor.matmul(v_psum[r][:, k // 2, W + k % 2:W + k % 2 + 1], hT[r][:, k * P:(k + 1) * P],
                                        wa[:, 0:1], start=True, stop=True)
            last.then_inc(projected, 1)
            if not (isinstance(c, int) and c == blocks - 1):
                transpose_h(c + 1, 1 - r)
            if first and not isinstance(c, int):
                if r == 0:
                    transpose_adj(i, SCALAR, i * 2 + 2)
            elif first and c == blocks - 4:
                transpose_adj(POOL_TILE, POOL, 2)
            elif first and c == blocks - 3:
                transpose_adj(3, SCALAR, 6)
            elif first and c == blocks - 1:
                transpose_adj(4, SCALAR, 8)
            pe.wait_ge(s_kept, c + 1)
            nc.tensor.matmul(pro[:, 1, :], wa1_rep, hT[r], start=True, stop=True).then_inc(s_psum, 1)

        def multiply_early(some_groups):
            pe.wait_ge(parts_ready, 2 * some_groups.stop)
            multiply(0, 0, 0, some_groups)

        def prologue():
            pe.wait_ge(w2_ready, 1)
            nc.tensor.matmul(pro[:, 0, 0:P], ones[:, :], squares, start=True, stop=True).then_inc(n2_ready, 1)
            yield
            if first:
                pe.sem_inc(transposed, 2)
            else:
                pe.wait_ge(before["combined"], tiles * 4 + 1)
            transpose_h(0, 0)
            yield
            pe.wait_ge(w2_ready, 7)
            if first:
                prologue_steps(pe, project)
            else:
                for c in range(blocks):
                    project(c, c // 2, c % 2)
                    if c == blocks - 3:
                        pe.wait_ge(before["h_ready"], tiles + 2)
                        multiply_early(range(1))
                    if c > blocks - 3:
                        multiply_early(early_groups(c - 1))
                    yield
            pe.wait_ge(head, 2)
            nc.tensor.matmul(pro[:, 0, 0:P], h_rep, w_sb, start=True, stop=True).then_inc(mean_psum, 1)

        masks_built = Ticks(pe, masks_ready, 1)
        sums_read = Ticks(pe, h_ready, 1)

        def multiply(b, r, k, group_range):
            if 0 in group_range:
                sums_read.wait(b * BLOCK_TILES + (k + 1))
            for g in group_range:
                if k == 0:
                    masks_built.wait(b * groups + (g + 1))
                for byte in range(BYTES):
                    j = BYTES * g + byte
                    for sign in range(2):
                        mask = masks[r][sign][:, g, k * P:(k + 1) * P].bitcast(FP8)\
                            .rearrange("p (i b) -> p b i", b=BYTES)[:, byte, :]
                        last = nc.tensor.matmul(acc[:, k % 2, sign, 0:W], mask, parts[:, j, sign, :],
                                                start=(j == 0), stop=(j == tiles - 1))
            if groups - 1 in group_range:
                last.then_inc(acc_done, 1)

        def transpose_next(b, k, transposing):
            if transposing:
                tile = b * BLOCK_TILES + (2 * BLOCK_TILES + k)
                if k == POOL_TILE:
                    transpose_adj(tile, POOL, b * 2 + 6)
                else:
                    transpose_adj(tile, SCALAR, b * 6 + 2 * (act_tile(2, k) + 1))

        def stage(b, r, transposing, ahead, building, multiplying, next_layer):
            if not multiplying:
                pe.wait_ge(ready, 1)
            for k in range(BLOCK_TILES):
                if next_layer and b == blocks - 2 and k == 2:
                    next(next_layer)
                in_middle = isinstance(b, int) and b == 0 and k == 1
                if multiplying and not in_middle:
                    transpose_next(b, k, transposing)
                if in_middle:
                    multiply(b, r, k, range(groups // 2))
                    transpose_next(b, k, transposing)
                    multiply(b, r, k, range(groups // 2, groups))
                elif not multiplying:
                    if k > 0:
                        transpose_next(b, k, transposing)
                    multiply(0, 0, 0, range(max(2 * k - 1, EARLY_GROUPS),
                                            2 * k + 1 if k < BLOCK_TILES - 1 else groups))
                elif isinstance(b, int) and b == 0 and k == 0:
                    pass
                elif next_layer and b == blocks - 1:
                    multiply(b, r, k, range(groups // 2))
                    if k > 0:
                        next(next_layer)
                    multiply(b, r, k, range(groups // 2, groups))
                    if k < BLOCK_TILES - 1:
                        next(next_layer)
                else:
                    multiply(b, r, k, range(groups))

        def run_stages(next_layer):
            pe.reg_mov(masks_built.value, groups + 1)
            pe.reg_mov(sums_read.value, BLOCK_TILES + 1)
            stages(pe, stage, next_layer)

        return prologue(), run_stages

    def scalar_program(act):
        def weight_norm():
            act.wait_ge(w2_ready, 3)
            nc.scalar.activation(root, n2, ACT.Sqrt).then_inc(root_ready, 1)

        def deviations(part):
            of = slice(LN_PARTS[part].start, LN_PARTS[part].stop)
            act.wait_ge(ln, part * LN_STEPS + 8)
            nc.scalar.activation(std[:, of], var[:, of], ACT.Sqrt).then_inc(std_ready, 1)

        def compare_for(b, r):
            def compare(g):
                below_t = masks[1 - r][1][:, g, :].bitcast(I8).rearrange("p (i b) -> p b i", b=BYTES)
                for byte in act_bytes[g % 2]:
                    j = BYTES * g + byte
                    nc.scalar.activation(below_t[:, byte, :], s_rows[:, bass.ds(b * BLOCK + BLOCK, BLOCK)],
                                         ACT.Sign, bias=t_all[:, j:j + 1]).then_inc(signed, 1)

            return compare

        def pack(m, tile_before, halves=(0, 1)):
            if 0 in halves:
                act.wait_ge(transposed, tile_before + 3)
            for h in halves:
                act.wait_ge(adj_in[SCALAR][h], m * 16 + 16)
                nc.scalar.activation(mem["bytes"][SCALAR][:, h * HALF // 4:(h + 1) * HALF // 4].bitcast(U8),
                                     mem["adj_sb"][SCALAR][h][:, :], ACT.Relu, bias=127.0, scale=-127.0)\
                    .then_inc(packed[SCALAR], 1)

        def relu(c, r):
            act.wait_ge(h_psum, c + 1)
            act.wait_ge(root_ready, 1)
            nc.scalar.activation(hT[r], pro[:, 0, :], ACT.Relu, accum_out=h_sum[:, bass.ds(c, 1)])\
                .then_inc(hT_ready, 1)

        def copy_out(c, i, r):
            act.wait_ge(projected, c + 1)
            nc.scalar.activation(v_sb[r], v_psum[r][:, :, 0:PAIR], ACT.Copy).then_inc(v_ready, 1)
            act.wait_ge(bounded, c + 1)
            for k, slope in enumerate((1.0, ALPHA)):
                nc.scalar.activation(exps[r][:, k, :], t_low[r], ACT.Exp, scale=slope).then_inc(exp_t, 1)
            if not (isinstance(c, int) and c == blocks - 1):
                relu(c + 1, 1 - r)
            if first:
                if not isinstance(c, int):
                    pack(i + 1, i, (r,))
                elif c in (blocks - 3, blocks - 2):
                    pack(3, 3, (c - (blocks - 3),))
                elif c == blocks - 1:
                    pack(4, 4, (0,))
            for k in range(2):
                act.wait_ge(v_scaled, c * 2 + (k + 1))
                act.wait_ge(root_ready, 1)
                nc.scalar.activation(parts[:, bass.ds(c * BYTES, BYTES), k, 0:P + 1], scaled[r][:, k, :, :],
                                     ACT.Copy, scale=1.0 / LOW_SCALE).then_inc(hi_ready, 1)
            act.wait_ge(s_psum, c + 1)
            act.wait_ge(root_ready, 1)
            nc.scalar.activation(s_rows[:, bass.ds(c * BLOCK, BLOCK)], pro[:, 1, :], ACT.Copy).then_inc(s_kept, 1)

        def prologue():
            weight_norm()
            deviations(0)
            act.sem_inc(s_kept, 1)
            act.sem_inc(v_ready, 2)
            yield
            relu(0, 0)
            if first:
                pack(0, -1)
                deviations(1)
            yield
            if first:
                prologue_steps(act, copy_out)
            else:
                act.wait_ge(before["masks_ready"], blocks * groups)
                compare = compare_for(-1, 1)
                for c in range(blocks):
                    if c == 3:
                        deviations(1)
                    if c == blocks - 3:
                        compare(0)
                        deviations(2)
                    copy_out(c, c // 2, c % 2)
                    if c >= blocks - 3:
                        for g in early_groups(c):
                            compare(g)
                    yield
            act.wait_ge(head, 3)
            nc.scalar.activation(w4[:, :, 0], s_neg, ACT.Exp).then_inc(row_exp, 1)
            act.wait_ge(head, 4)
            nc.scalar.activation(w4[:, :, 2], tmp, ACT.Exp).then_inc(row_exp, 1)

        def stage(b, r, transposing, ahead, building, multiplying, next_layer):
            if not multiplying:
                act.wait_ge(ready, 1)

            compare_all = compare_for(b, r)

            def compare(g):
                if building and (EARLY_GROUPS if not multiplying else 0) <= g < groups:
                    compare_all(g)

            def pack_tile(k, halves=(0, 1)):
                tile = b * BLOCK_TILES + (2 * BLOCK_TILES + k)
                pack(b * 3 + act_tile(2, k), tile - (2 if k == 3 else 1), halves)

            compare(0)
            if transposing:
                pack_tile(1, (1,))
            compare(1)
            compare(2)
            for k in range(BLOCK_TILES):
                tile = b * BLOCK_TILES + k
                if multiplying:
                    act.wait_ge(den_steps, tile * 6 + 3)
                    nc.scalar.activation(fill, mean_rep, ACT.Copy, scale=flag).then_inc(fill_ready, 1)
                if ahead and k == 2 and multiplying:
                    pack_tile(BLOCK_TILES)
                if ahead and k == 3:
                    pack_tile(BLOCK_TILES + 1, (0,))
                if transposing and k < 2 and not multiplying:
                    pack_tile(3, (k,))
                compare(2 * k + 3)
                compare(2 * k + 4)
                if transposing and k < 2 and multiplying:
                    pack_tile(3, (k,))
                if ahead and k == 2 and not multiplying:
                    pack_tile(BLOCK_TILES)
                if multiplying:
                    act.wait_ge(h_ready, tile + 3)
                    nc.scalar.activation(e_buf, h_buf, ACT.Relu, scale=-1.0).then_inc(e_neg, 1)
                    act.wait_ge(e_neg, tile + 1)
                    nc.scalar.activation(e_buf, e_buf, ACT.Exp, scale=-1.0).then_inc(e_ready, 1)
                if next_layer and b == blocks - 2 and k == BLOCK_TILES - 1:
                    next(next_layer)
                if next_layer and b == blocks - 1 and k < BLOCK_TILES - 1:
                    for part in range(2):
                        next(next_layer)
                if building or multiplying:
                    act.wait_ge(ready, 1)

        return prologue(), lambda next_layer: stages(act, stage, next_layer)

    def vector_program(dve):
        def square_weights():
            dve.wait_ge(loaded, 32)
            nc.vector.tensor_tensor(squares, w_sb, w_sb, ALU.mult).then_inc(w2_ready, 1)

        def largest_norm():
            dve.wait_ge(n2_ready, 1)
            nc.vector.reduce_max(n2, pro[:, 0, 0:P], AX.X).then_inc(w2_ready, 1)
            dve.wait_ge(w2_ready, 2)
            nc.vector.tensor_scalar(mem["bad"][:, 2 * layer:2 * layer + 1], n2, HUGE, None, ALU.is_le)
            nc.vector.tensor_scalar(n2, n2, TINY, None, ALU.max).then_inc(w2_ready, 1)

        def weights():
            nc.vector.tensor_tensor(products, a_rep.rearrange("p (c f) -> p c f", c=2),
                                    w_sb.unsqueeze(1).broadcast_to([P, 2, P]), ALU.mult).then_inc(w2_ready, 1)
            dve.wait_ge(w2_ready, 4)
            nc.vector.reduce_sum(wa, products, AX.X).then_inc(w2_ready, 1)
            for g in range(groups):
                nc.vector.memset(gains[:, BYTES * g:BYTES * (g + 1)], LOW_SCALE * BIT_VALUE[0] / BIT_VALUE[g % 4])
            dve.wait_ge(root_ready, 1)
            nc.vector.reciprocal(c_v, root).then_inc(w2_ready, 1)
            nc.vector.tensor_scalar(k_v, root, DEN_UNIT / V_BOUND, None, ALU.mult)
            dve.wait_ge(w2_ready, 6)
            nc.vector.tensor_scalar(wx[:, 0:P], w_sb, c_v, V_BOUND, ALU.mult, ALU.mult)
            nc.vector.tensor_copy(wx[:, P:P + 1], wa[:, 1:2])
            nc.vector.tensor_copy(wa1_rep, wa[:, 0:1].broadcast_to([P, P])).then_inc(w2_ready, 1)

        def statistics(row_tiles, part=None):
            for t in row_tiles:
                if first and t % (tiles // X_PARTS) == 0:
                    dve.wait_ge(x_loaded[t * X_PARTS // tiles], 16)
                if before:
                    dve.wait_ge(before["x_done"], t + 1)
                last = nc.vector.bn_stats(stats[:, t, :], x_sb[:, t, :])
            if part is not None:
                last.then_inc(ln, 1)

        def layer_norm(part, meanwhile=None):
            of, base = slice(LN_PARTS[part].start, LN_PARTS[part].stop), part * LN_STEPS
            me, m2e, mo, m2o = (stats[:, of, q] for q in (1, 2, 4, 5))
            mean_, tmp_, var_, std_, rstd_ = (buf[:, of] for buf in (mean, tmp, var, std, rstd))
            dve.wait_ge(ln, base + 1)
            nc.vector.tensor_tensor(mean_, me, mo, ALU.add).then_inc(ln, 1)
            nc.vector.tensor_tensor(tmp_, me, mo, ALU.subtract).then_inc(ln, 1)
            nc.vector.tensor_tensor(var_, m2e, m2o, ALU.add).then_inc(ln, 1)
            dve.wait_ge(ln, base + 4)
            nc.vector.tensor_scalar(mean_, mean_, 0.5, None, ALU.mult).then_inc(ln, 1)
            nc.vector.tensor_tensor(tmp_, tmp_, tmp_, ALU.mult).then_inc(ln, 1)
            dve.wait_ge(ln, base + 6)
            nc.vector.scalar_tensor_tensor(var_, tmp_, P / 4.0, var_, ALU.mult, ALU.add).then_inc(ln, 1)
            dve.wait_ge(ln, base + 7)
            nc.vector.tensor_scalar(var_, var_, 1.0 / P, EPS, ALU.mult, ALU.add).then_inc(ln, 1)
            if meanwhile is not None:
                meanwhile()
            dve.wait_ge(std_ready, part + 1)
            nc.vector.reciprocal(rstd_, std_).then_inc(ln, 1)
            dve.wait_ge(ln, base + 9)
            nc.vector.tensor_tensor(tmp_, rstd_, rstd_, ALU.mult).then_inc(ln, 1)
            dve.wait_ge(ln, base + 10)
            nc.vector.tensor_tensor(tmp_, tmp_, var_, ALU.mult).then_inc(ln, 1)
            dve.wait_ge(ln, base + 11)
            nc.vector.tensor_scalar(tmp_, tmp_, -0.5, 1.5, ALU.mult, ALU.add).then_inc(ln, 1)
            dve.wait_ge(ln, base + 12)
            nc.vector.tensor_tensor(rstd_, rstd_, tmp_, ALU.mult).then_inc(ln, 1)
            dve.wait_ge(ln, base + LN_STEPS)

        def mask_steps(b, r):
            nxt = b * groups + groups
            rows = bass.ds(b * BLOCK + BLOCK, BLOCK)

            def compare(g):
                below_t = masks[1 - r][1][:, g, :].bitcast(U8).rearrange("p (i b) -> p b i", b=BYTES)
                for byte in dve_bytes[g % 2]:
                    j = BYTES * g + byte
                    nc.vector.tensor_scalar(below_t[:, byte, :], s_rows[:, rows], neg_t[:, j:j + 1],
                                            float(BITS[g % 4]), ALU.is_lt, ALU.mult).then_inc(below, 1)

            def cut_neg(g):
                neg = masks[1 - r][1][:, g, :]
                dve.wait_ge(below, compared(dve_bytes, b + 1, g))
                dve.wait_ge(signed, compared(act_bytes, b + 1, g))
                nc.vector.scalar_tensor_tensor(neg, neg, word(BITS[g % 4]), bits[:, g // 4, rows],
                                               ALU.bitwise_and, ALU.bitwise_and).then_inc(neg_ready, 1)

            def cut_pos(g):
                dve.wait_ge(neg_ready, nxt + (g + 1))
                nc.vector.scalar_tensor_tensor(masks[1 - r][0][:, g, :], bits[:, g // 4, rows],
                                               word(BITS[g % 4]), masks[1 - r][1][:, g, :],
                                               ALU.bitwise_and, ALU.bitwise_xor).then_inc(masks_ready, 1)

            return compare, cut_neg, cut_pos

        def normalise(c, r):
            for k in range(BLOCK_TILES):
                t = c * BLOCK_TILES + k
                last = nc.vector.tensor_scalar(norm[r][:, k * P:(k + 1) * P],
                                               x_sb[:, bass.ds(t, 1), :].rearrange("p t f -> p (t f)"),
                                               mean[:, bass.ds(t, 1)], rstd[:, bass.ds(t, 1)],
                                               ALU.subtract, ALU.mult)
            last.then_inc(norm_ready, 1)

        def combine(tile, step):
            where = bits[:, :, bass.ds(tile * P, P)]
            came = tr[:, step::4, :].bitcast(U32)
            if step == 0:
                dve.wait_ge(transposed, tile + 3)
                nc.vector.tensor_scalar(where, came, word(BITS[0]), ALL_BITS, ALU.bitwise_and, ALU.bitwise_xor)\
                    .then_inc(combined, 1)
            else:
                dve.wait_ge(combined, tile * 4 + (step + 1))
                nc.vector.scalar_tensor_tensor(where, came, word(BITS[step]), where, ALU.bitwise_and,
                                               ALU.bitwise_xor).then_inc(combined, 1)

        def split(c, i, r):
            j = c * BYTES
            t_of = v_sb[r][:, :, P:2 * (P + 1):P + 1]
            dve.wait_ge(v_ready, c + 3)
            nc.vector.tensor_scalar(t_low[r].rearrange("p (a b) -> p a b", a=2), t_of, T_MAX, -T_MAX,
                                    ALU.min, ALU.max).then_inc(bounded, 1)
            nc.vector.tensor_copy(s_col[:, bass.ds(c * BLOCK_TILES, BLOCK_TILES)].rearrange("p (a b) -> p a b", a=2),
                                  v_sb[r][:, :, W:W + 2])
            nc.vector.tensor_copy(t_all[:, bass.ds(j, BYTES)].rearrange("p (a b) -> p a b", a=2), t_of)
            if not isinstance(c, int) or c < (blocks - 2 if first else blocks - 3):
                normalise(c + 2, r)
            dve.wait_ge(exp_t, c * 2 + 2)
            nc.vector.tensor_tensor(exps[r], exps[r], gains[:, bass.ds(j, BYTES)].unsqueeze(1)
                                    .broadcast_to([P, 2, BYTES]), ALU.mult).then_inc(gained, 1)
            dve.wait_ge(gained, c + 1)
            nc.vector.tensor_scalar(scaled[r][:, :, :, P], exps[r], DEN_UNIT, None, ALU.mult)
            v_of = v_sb[r][:, :, 0:2 * (P + 1)].rearrange("p a (b f) -> p a b f", b=2)[:, :, :, 0:P]
            for k in range(2):
                nc.vector.tensor_tensor(scaled[r][:, k, :, 0:P].rearrange("p (a b) f -> p a b f", a=2), v_of,
                                        exps[r][:, k, :].rearrange("p (a b) -> p a b", a=2).unsqueeze(3)
                                        .broadcast_to([P, 2, 2, P]), ALU.mult).then_inc(v_scaled, 1)
            tile = i if not isinstance(c, int) else {blocks - 4: POOL_TILE, blocks - 3: 3, blocks - 1: 4}.get(c)
            if first and (r == 0 if not isinstance(c, int) else tile is not None):
                for step in range(4):
                    combine(tile, step)
            for k in range(2):
                dve.wait_ge(hi_ready, c * 2 + (k + 1))
                nc.vector.scalar_tensor_tensor(parts[:, bass.ds(j, BYTES), k, P + 1:W],
                                               parts[:, bass.ds(j, BYTES), k, 0:P + 1], -LOW_SCALE,
                                               scaled[r][:, k, :, :], ALU.mult, ALU.add).then_inc(parts_ready, 1)
            if EARLY_GROUPS:
                nc.vector.tensor_scalar(neg_t[:, j:j + BYTES], t_all[:, j:j + BYTES], -1.0, None, ALU.mult)

        def prologue():
            dve.sem_inc(h_ready, 2)
            if first:
                square_weights()
                largest_norm()
                weights()
                dve.sem_inc(combined, 1)
                statistics(LN_PARTS[0], 0)
                layer_norm(0)
                for c in range(2):
                    normalise(c, c)
                statistics(LN_PARTS[1], 1)
                layer_norm(1)
                prologue_steps(dve, split)
            else:
                square_weights()
                statistics(range(0, 10))
                yield
                statistics(range(10, LN_PARTS[0].stop), 0)
                yield
                largest_norm()
                yield
                layer_norm(0)
                yield
                dve.wait_ge(before["acc_done"], (blocks - 1) * BLOCK_TILES)
                for c in range(2):
                    normalise(c, c)
                weights()
                yield
                compare, cut_neg, cut_pos = mask_steps(-1, 1)

                def build(*some_groups):
                    for g in some_groups:
                        compare(g)
                        cut_neg(g)
                        cut_pos(g)

                for c in range(blocks):
                    if c == 3:
                        statistics(LN_PARTS[1], 1)
                        layer_norm(1)
                    if c == blocks - 3:
                        statistics(LN_PARTS[2], 2)
                        layer_norm(2, lambda: build(0))
                        normalise(blocks - 1, 1)
                    split(c, c // 2, c % 2)
                    if c >= blocks - 3:
                        build(*early_groups(c))
                    yield
            finish_prologue()

        def finish_prologue():
            dve.wait_ge(hT_ready, blocks)
            nc.vector.reduce_sum(h_total, h_sum, AX.X).then_inc(head, 1)
            dve.wait_ge(head, 1)
            nc.vector.tensor_scalar(h_rep, h_total.broadcast_to([P, P]), 1.0 / n, None, ALU.mult).then_inc(head, 1)
            dve.wait_ge(parts_ready, 2 * blocks)
            if not EARLY_GROUPS:
                nc.vector.tensor_scalar(neg_t, t_all, -1.0, None, ALU.mult)
            nc.vector.tensor_scalar(s_neg, s_col, 1.0 - ALPHA, 0.0, ALU.mult, ALU.min).then_inc(head, 1)
            nc.vector.tensor_scalar(tmp, s_col, ALPHA - 1.0, 0.0, ALU.mult, ALU.min).then_inc(head, 1)
            nc.vector.scalar_tensor_tensor(mean, t_all, -1.0, t_all, ALU.mult, ALU.max).then_inc(head, 1)
            dve.wait_ge(head, 5)
            nc.vector.tensor_scalar(mean, mean, T_MAX, None, ALU.is_le).then_inc(head, 1)
            dve.wait_ge(head, 6)
            nc.vector.tensor_reduce(mem["bad"][:, 2 * layer + 1:2 * layer + 2], mean, axis=AX.X, op=ALU.min)\
                .then_inc(head, 1)
            dve.wait_ge(mean_psum, 1)
            nc.vector.tensor_copy(mean_rep, pro[:, 0, 0:P])
            dve.wait_ge(row_exp, 2)
            nc.vector.tensor_scalar(w4[:, :, 1], w4[:, :, 0], 1.0 / LOW_SCALE, None, ALU.mult).then_inc(head, 1)
            nc.vector.tensor_scalar(w4[:, :, 3], w4[:, :, 2], 1.0 / LOW_SCALE, None, ALU.mult).then_inc(head, 1)
            dve.wait_ge(head, 9)
            nc.vector.tensor_scalar(w4k, w4, k_v, None, ALU.mult).then_inc(ready, 1)

    
        def stage(b, r, transposing, ahead, building, multiplying, next_layer):

            compare, cut_neg, cut_pos = mask_steps(b, r)

            def row(k):
                return b * BLOCK_TILES + k

            def weigh_sums(k):
                dve.wait_ge(acc_done, row(k) + 1)
                w_t = w4[:, bass.ds(row(k), 1), :].rearrange("p t (a b) -> p (t a) b", a=2)
                nc.vector.tensor_tensor(den4.rearrange("p (a b) -> p a b", a=2), acc[:, k % 2, :, P:W:P + 1], w_t,
                                        ALU.mult).then_inc(den_steps, 1)

            def add_sums(k):
                dve.wait_ge(den_steps, row(k) * 6 + 1)
                nc.vector.reduce_sum(den, den4, AX.X).then_inc(den_steps, 1)

            def guard(k):
                dve.wait_ge(den_steps, row(k) * 6 + 2)
                nc.vector.tensor_scalar(flag, den, 0.0, None, ALU.is_equal).then_inc(den_steps, 1)
                nc.vector.tensor_scalar(den, den, TINY, None, ALU.max).then_inc(den_steps, 1)

            def invert(k):
                dve.wait_ge(den_steps, row(k) * 6 + 4)
                nc.vector.reciprocal(rec, den).then_inc(den_steps, 1)

            def row_factors(k):
                wk_t = w4k[:, bass.ds(row(k), 1), :].rearrange("p t k -> p (t k)")
                dve.wait_ge(den_steps, row(k) * 6 + 5)
                nc.vector.tensor_scalar(w4r, wk_t, rec, None, ALU.mult).then_inc(den_steps, 1)

            def average(k, m):
                o = (m % 2) * (P + 1)
                if m == 0:
                    dve.wait_ge(den_steps, row(k) * 6 + 6)
                    dve.wait_ge(fill_ready, row(k) + 1)
                else:
                    dve.wait_ge(h_steps, row(k) * 3 + m)
                nc.vector.scalar_tensor_tensor(h_buf, acc[:, k % 2, m // 2, o:o + P], w4r[:, m:m + 1],
                                               h_buf if m else fill, ALU.mult, ALU.add)\
                    .then_inc(h_steps if m < 3 else h_ready, 1)

            def elu(k):
                dve.wait_ge(e_ready, row(k) + 1)
                nc.vector.scalar_tensor_tensor(e_buf, e_buf, -1.0, h_buf, ALU.add, ALU.max).then_inc(up_ready, 1)

            def update(k):
                x_t = x_sb[:, bass.ds(row(k), 1), :].rearrange("p t f -> p (t f)")
                dve.wait_ge(up_ready, row(k) + 1)
                nc.vector.tensor_tensor(x_t, x_t, e_buf, ALU.add).then_inc(x_done, 1)

            def build(g, *steps):
                if building and (EARLY_GROUPS if not multiplying else 0) <= g < groups:
                    for step in steps:
                        step(g)

            def combine_tile(k, step):
                if transposing if k < BLOCK_TILES else ahead:
                    combine(b * BLOCK_TILES + (2 * BLOCK_TILES + k), step)

            unfinished = multiplying and not (isinstance(b, int) and b == 0)
            build(0, compare)
            if unfinished:
                elu(-1)
            build(0, cut_neg)
            if unfinished:
                update(-1)
            build(0, cut_pos)
            if next_layer and b == blocks - 1:
                next(next_layer)
            for k in range(BLOCK_TILES):
                g = 2 * k + 1
                if multiplying:
                    weigh_sums(k)
                build(g, compare)
                if multiplying:
                    add_sums(k)
                    if k:
                        elu(k - 1)
                    guard(k)
                    if k:
                        update(k - 1)
                    invert(k)
                build(g, cut_neg)
                if multiplying:
                    row_factors(k)
                late = not multiplying
                if not late:
                    combine_tile(k + 1, 0)
                for m in range(4):
                    if multiplying:
                        average(k, m)
                    if m < 3 and not late:
                        combine_tile(k + 1, m + 1)
                build(g, cut_pos)
                build(g + 1, compare, cut_neg, cut_pos)
                if late:
                    for step in range(4):
                        combine_tile(k + 1, step)
                if next_layer:
                    for part in range(1 if b == blocks - 2 or k == 0 else 2 if k < BLOCK_TILES - 1 else 0):
                        next(next_layer)
            if isinstance(b, int) and b == blocks - 1:
                elu(BLOCK_TILES - 1)
                update(BLOCK_TILES - 1)

        return prologue(), lambda next_layer: stages(dve, stage, next_layer)

    return {"sync": sync, "gpsimd": gpsimd, "tensor": tensor_program, "scalar": scalar_program, "vector": vector_program,
            "transposed": transposed, "combined": combined, "acc_done": acc_done, "masks_ready": masks_ready,
            "x_done": x_done, "h_ready": h_ready}


def fast_path(nc, x_in, adj, weights, out, mems):
    with ExitStack() as ctx:
        one = fast_layer(ctx, nc, 0, x_in, adj, *weights[0], out, mems[0])
        two = fast_layer(ctx, nc, 1, x_in, adj, *weights[1], out, mems[1], one)

        def both(name, eng):
            prologue, run_stages = one[name](eng)
            next_layer, run_next_stages = two[name](eng)
            for _ in prologue:
                pass
            run_stages(next_layer)
            for _ in next_layer:
                pass
            run_next_stages(None)

        with nc.Block() as block:
            @block.sync
            def _(sp):
                one["sync"](sp)
                two["sync"](sp)

            @block.gpsimd
            def _(pool):
                one["gpsimd"](pool)

            @block.tensor
            def _(pe):
                both("tensor", pe)

            @block.scalar
            def _(act):
                both("scalar", act)

            @block.vector
            def _(dve):
                both("vector", dve)


def general_layer(nc, layer, x_in, adj, w_in, a_in, out, x_sb, ident, room, psum):
    n = adj.shape[0]
    tiles = n // P
    with ExitStack() as ctx:
        def sem(name):
            return ctx.enter_context(nc.semaphore(f"general{layer}_{name}"))

        at = [0, 0]

        def take(words, part=1):
            at[part] += words
            return room[part][:, at[part] - words:at[part]]

        adj_tile = take(n, 0).bitcast(I32)
        score = take(n, 0)
        prob = take(n, 0)
        t_rows = take(n, 0)
        v_all = take(n, 0).rearrange("p (t f) -> p t f", f=P)
        probT = take(n, 0).rearrange("p (t i) -> p t i", i=P)
        w_ext = take(P + 2)
        a_rep = take(2 * P)
        products = take(2 * P)
        wa2_rep = take(P)
        s_all = take(tiles)
        norm_tile = take(P)
        hT = take(P)
        norm = score.rearrange("p (t f) -> p t f", f=P)
        squares = prob.rearrange("p (t f) -> p t f", f=P)
        out_tile = take(P)
        pos = take(P)
        neg = take(P)
        mean = take(tiles)
        var = take(tiles)
        std = take(tiles)
        rstd = take(tiles)
        tmp = take(tiles)
        row_max = take(1)
        neg_max = take(1)
        row_sum = take(1)
        recip = take(1)
        _, psH, psV, psT, psP, psO = psum[0], psum[1], psum[2], psum[3], psum[4:6], psum[6]

        loaded = sem("loaded")
        wa_steps = sem("wa_steps")
        ln = sem("ln")
        norm_ready = sem("norm_ready")
        std_ready = sem("std_ready")
        h_transposed = sem("h_transposed")
        hT_ready = sem("hT_ready")
        projected = sem("projected")
        kept = sem("kept")
        adj_loaded = sem("adj_loaded")
        sc = sem("sc")
        exp_done = sem("exp_done")
        p_transposed = sem("p_transposed")
        probT_ready = sem("probT_ready")
        product = sem("product")
        ep = sem("ep")
        elu_exp = sem("elu_exp")
        stored = sem("stored")

        SC_STEPS, EP_STEPS = 8, 6
        groups = tiles // 4

        with nc.Block() as block:
            @block.gpsimd
            def _(pool):
                if layer == 0:
                    pool.dma_start(x_sb[:, :, :], x_in.rearrange("(t p) f -> p t f", p=P)).then_inc(loaded, 16)
                pool.dma_start(w_ext[:, 0:P], w_in).then_inc(loaded, 16)
                pool.dma_start(a_rep, a_in.rearrange("c o -> o c").broadcast_to([P, 2 * P])).then_inc(loaded, 16)

            @block.sync
            def _(sp):
                with sp.Fori(0, tiles) as i:
                    sp.wait_ge(sc, i * SC_STEPS + 1)
                    sp.dma_start(adj_tile, adj[bass.ts(i, P), :]).then_inc(adj_loaded, 16)
                if layer == 1:
                    sp.wait_ge(ep, tiles * EP_STEPS + 1)
                    sp.dma_start(out.rearrange("(t p) f -> p t f", p=P), x_sb[:, :, :]).then_inc(stored, 16)
                    sp.wait_ge(stored, 16)

            @block.tensor
            def _(pe):
                pe.wait_ge(loaded, 48 if layer == 0 else 32)
                pe.wait_ge(wa_steps, 4)
                with pe.Fori(0, tiles) as i:
                    pe.wait_ge(norm_ready, i + 1)
                    nc.tensor.transpose(psH[:, 0:P], norm_tile, ident[:, :]).then_inc(h_transposed, 1)
                    pe.wait_ge(hT_ready, i + 1)
                    nc.tensor.matmul(psV[:, 0:P + 2], hT, w_ext, start=True, stop=True)
                    nc.tensor.matmul(psT[:, 0:P], wa2_rep, hT, start=True, stop=True).then_inc(projected, 1)
                pe.sem_inc(product, 1)
                with pe.Fori(0, tiles) as i:
                    pe.wait_ge(exp_done, i + 1)
                    for g in range(groups):
                        if g < 2:
                            pe.wait_ge(probT_ready, i * groups + 1)
                        else:
                            pe.wait_ge(probT_ready, i * groups + g)
                        for k in range(4):
                            j = 4 * g + k
                            last = nc.tensor.transpose(psP[g % 2][:, k * P:(k + 1) * P],
                                                       prob[:, j * P:(j + 1) * P], ident[:, :])
                        last.then_inc(p_transposed, 1)
                    pe.wait_ge(probT_ready, i * groups + (groups + 1))
                    pe.wait_ge(ep, i * EP_STEPS + 1)
                    for j in range(tiles):
                        last = nc.tensor.matmul(psO[:, 0:P], probT[:, j, :], v_all[:, j, :],
                                                start=(j == 0), stop=(j == tiles - 1))
                    last.then_inc(product, 1)

            @block.scalar
            def _(act):
                act.wait_ge(ln, 6)
                nc.scalar.activation(std, var, ACT.Sqrt).then_inc(std_ready, 1)
                with act.Fori(0, tiles) as i:
                    act.wait_ge(h_transposed, i + 1)
                    nc.scalar.activation(hT, psH[:, 0:P], ACT.Relu).then_inc(hT_ready, 1)
                act.sem_inc(probT_ready, 1)
                with act.Fori(0, tiles) as i:
                    act.wait_ge(sc, i * SC_STEPS + (SC_STEPS + 1))
                    nc.scalar.activation(prob, score, ACT.Exp, bias=neg_max, accum_out=row_sum).then_inc(exp_done, 1)
                    act.wait_ge(product, i + 1)
                    for g in range(groups):
                        act.wait_ge(p_transposed, i * groups + (g + 1))
                        nc.scalar.activation(probT[:, 4 * g:4 * g + 4, :], psP[g % 2][:, 0:4 * P].rearrange("p (t i) -> p t i", i=P),
                                             ACT.Copy).then_inc(probT_ready, 1)
                    act.wait_ge(ep, i * EP_STEPS + 4)
                    nc.scalar.activation(neg, neg, ACT.Exp).then_inc(elu_exp, 1)

            @block.vector
            def _(dve):
                def run(count, base, signal, ops):
                    for k, op in enumerate(ops):
                        op().then_inc(signal, 1)
                        dve.wait_ge(signal, base + (count + k + 1))

                dve.wait_ge(loaded, 48 if layer == 0 else 32)
                for c in range(2):
                    nc.vector.tensor_tensor(products[:, c * P:(c + 1) * P], w_ext[:, 0:P], a_rep[:, c * P:(c + 1) * P],
                                            ALU.mult).then_inc(wa_steps, 1)
                dve.wait_ge(wa_steps, 2)
                nc.vector.reduce_sum(w_ext[:, P:P + 2], products.rearrange("p (c f) -> p c f", c=2), AX.X).then_inc(wa_steps, 1)
                dve.wait_ge(wa_steps, 3)
                nc.vector.tensor_copy(wa2_rep, w_ext[:, P + 1:P + 2].broadcast_to([P, P])).then_inc(wa_steps, 1)
                per_row = lambda v: v.unsqueeze(2).broadcast_to([P, tiles, P])
                run(0, 0, ln, [
                    lambda: nc.vector.reduce_sum(mean, x_sb[:, :, :], AX.X),
                    lambda: nc.vector.tensor_scalar(mean, mean, 1.0 / P, None, ALU.mult),
                    lambda: nc.vector.tensor_tensor(norm, x_sb[:, :, :], per_row(mean), ALU.subtract),
                    lambda: nc.vector.tensor_tensor(squares, norm, norm, ALU.mult),
                    lambda: nc.vector.reduce_sum(var, squares, AX.X),
                    lambda: nc.vector.tensor_scalar(var, var, 1.0 / P, EPS, ALU.mult, ALU.add)])
                dve.wait_ge(std_ready, 1)
                run(6, 0, ln, [
                    lambda: nc.vector.reciprocal(rstd, std),
                    lambda: nc.vector.tensor_tensor(tmp, rstd, rstd, ALU.mult),
                    lambda: nc.vector.tensor_tensor(tmp, tmp, var, ALU.mult),
                    lambda: nc.vector.tensor_scalar(tmp, tmp, -0.5, 1.5, ALU.mult, ALU.add),
                    lambda: nc.vector.tensor_tensor(rstd, rstd, tmp, ALU.mult),
                    lambda: nc.vector.tensor_tensor(norm, norm, per_row(rstd), ALU.mult)])
                with dve.Fori(0, tiles) as i:
                    nc.vector.tensor_copy(norm_tile, score[:, bass.ts(i, P)]).then_inc(norm_ready, 1)
                    dve.wait_ge(projected, i + 1)
                    nc.vector.tensor_copy(v_all[:, bass.ds(i, 1), :].rearrange("p t f -> p (t f)"), psV[:, 0:P])
                    nc.vector.tensor_copy(s_all[:, bass.ds(i, 1)], psV[:, P:P + 1])
                    nc.vector.tensor_copy(t_rows[:, bass.ts(i, P)], psT[:, 0:P]).then_inc(kept, 1)
                    dve.wait_ge(kept, i + 1)
                dve.sem_inc(sc, 1)
                dve.sem_inc(ep, 1)
                with dve.Fori(0, tiles) as i:
                    base = i * SC_STEPS + 1
                    dve.wait_ge(adj_loaded, i * 16 + 16)
                    dve.wait_ge(product, i + 1)
                    run(0, base, sc, [
                        lambda: nc.vector.tensor_scalar(score, t_rows, s_all[:, bass.ds(i, 1)], None, ALU.add),
                        lambda: nc.vector.scalar_tensor_tensor(score, score, ALPHA, score, ALU.mult, ALU.max),
                        lambda: nc.vector.tensor_scalar(prob, adj_tile, 0, None, ALU.is_gt),
                        lambda: nc.vector.tensor_tensor(score, score, prob, ALU.mult),
                        lambda: nc.vector.tensor_scalar(prob, prob, 1.0, MASKED, ALU.subtract, ALU.mult),
                        lambda: nc.vector.tensor_tensor(score, score, prob, ALU.add),
                        lambda: nc.vector.reduce_max(row_max, score, AX.X),
                        lambda: nc.vector.tensor_scalar(neg_max, row_max, -1.0, None, ALU.mult)])
                    dve.wait_ge(exp_done, i + 1)
                    dve.wait_ge(product, i + 2)
                    base_e = i * EP_STEPS + 1
                    run(0, base_e, ep, [
                        lambda: nc.vector.reciprocal(recip, row_sum),
                        lambda: nc.vector.tensor_scalar(out_tile, psO[:, 0:P], recip, None, ALU.mult),
                        lambda: nc.vector.tensor_scalar(neg, out_tile, 0.0, None, ALU.min)])
                    run(3, base_e, ep, [
                        lambda: nc.vector.tensor_scalar(pos, out_tile, 0.0, -1.0, ALU.max, ALU.add)])
                    dve.wait_ge(elu_exp, i + 1)
                    x_t = x_sb[:, bass.ds(i, 1), :].rearrange("p t f -> p (t f)")
                    run(4, base_e, ep, [
                        lambda: nc.vector.tensor_tensor(pos, pos, neg, ALU.add),
                        lambda: nc.vector.tensor_tensor(x_t, x_t, pos, ALU.add)])


def build(nc, x, adj, w0, a0, w1, a1, out):
    n = adj.shape[0]
    tiles = n // P
    with ExitStack() as ctx:
        def sb(name, shape, dtype):
            return ctx.enter_context(nc.sbuf_tensor(name, shape, dtype))

        def sem(name):
            return ctx.enter_context(nc.semaphore(name))

        mem = {
            "x_sb": sb("x_sb", [P, tiles, P], F32),
            "s_rows": sb("s_rows", [P, n], F32),
            "bits": sb("bits", [P, 2, n], U32),
            "parts": sb("parts", [P, tiles, 2, 2 * (P + 1)], F16),
            "ident": sb("ident", [P, P], F32),
            "ones": sb("ones", [P, P], F32),
            "small": sb("small", [P, 1200], F32),
            "bad": sb("bad", [P, 4], F32),
        }
        verdict = sb("verdict", [P, 2], F32)
        verdict_int = sb("verdict_int", [1, 1], I32)
        room = sb("room", [P, 2 * 2 * n + 2 * n + 2 * n // 4], F32)
        masks = [[room[:, (2 * r + k) * n:(2 * r + k + 1) * n].bitcast(U32).rearrange("p (g i) -> p g i", i=BLOCK)
                  for k in range(2)] for r in range(2)]
        mem["masks"] = masks
        half = n // 2
        mem["adj_sb"] = [[room[:, 4 * n + (2 * r + h) * half:4 * n + (2 * r + h + 1) * half].bitcast(I32)
                          for h in range(2)] for r in range(2)]
        byte_room = room[:, 4 * n + 4 * half:]
        mem["bytes"] = [byte_room[:, r * n // 4:(r + 1) * n // 4] for r in range(2)]
        parts_words = tiles * 2 * (P + 1)
        after_parts = room[:, 4 * n + parts_words:]
        small_words = 1200
        mem["early"] = masks[1][0][:, :, :].rearrange("p q i -> p (q i)").bitcast(F32)[:, 6 * BLOCK:]
        mem1 = dict(mem)
        mem1["masks"] = [masks[1], masks[0]]
        mem1["parts"] = room[:, 4 * n:4 * n + parts_words].bitcast(F16)\
            .rearrange("p (t k c) -> p t k c", t=tiles, k=2)
        mem1["small"] = after_parts[:, 0:small_words]
        mem1["early"] = after_parts[:, small_words:]
        psum = ctx.enter_context(nc.psum_tensor("psum", [P, 8, 512], F32))
        mem["acc"] = psum[:, 0:4, :].rearrange("p (r s) c -> p r s c", r=2)
        mem["tr"] = psum[:, 4:6, :].rearrange("p b (w i) -> p (b w) i", i=P)
        mem["tr_banks"] = psum[:, 4:6, :]
        mem["pro"] = psum[:, 6:8, :]
        for name in ("acc", "tr", "tr_banks", "pro"):
            mem1[name] = mem[name]

        zeroed, made = sem("zeroed"), sem("made")
        with nc.Block() as block:
            @block.gpsimd
            def _(pool):
                nc.gpsimd.memset(mem["ones"][:, :], 1.0).then_inc(made, 1)
                nc.gpsimd.memset(mem["ident"][:, :], 0.0).then_inc(zeroed, 1)
                pool.wait_ge(zeroed, 1)
                nc.gpsimd.affine_select(out=mem["ident"][:, :], in_=mem["ident"][:, :], compare_op=ALU.not_equal, fill=1.0,
                                        base=0, pattern=[[-1, P]], channel_multiplier=1).then_inc(made, 1)
                pool.wait_ge(made, 2)

        fast_path(nc, x, adj, ((w0, a0), (w1, a1)), out, (mem, mem1))

        checks, counted, judged = sem("checks"), sem("counted"), sem("judged")
        with nc.Block() as block:
            @block.vector
            def _(dve):
                nc.vector.tensor_reduce(verdict[:, 0:1], mem["bad"][:, :], axis=AX.X, op=ALU.min).then_inc(checks, 1)
                dve.wait_ge(checks, 1)
                nc.vector.tensor_scalar(verdict[:, 1:2], verdict[:, 0:1], -1.0, 1.0, ALU.mult, ALU.add).then_inc(checks, 1)
                dve.wait_ge(counted, 1)
                nc.vector.tensor_copy(verdict_int[:, :], psum[0:1, 6, 0:1]).then_inc(judged, 1)
                dve.wait_ge(judged, 1)

            @block.tensor
            def _(pe):
                pe.wait_ge(checks, 2)
                nc.tensor.matmul(psum[0:1, 6, 0:1], verdict[:, 1:2], mem["ones"][:, 0:1], start=True, stop=True)\
                    .then_inc(counted, 1)

        failed = nc.values_load(verdict_int[0:1, 0:1], min_val=0, max_val=P)
        with nc.If(failed > 0):
            banks = [psum[:, b, :] for b in range(8)]
            general_room = [room[:, :], mem["bits"][:, :, :].rearrange("p a b -> p (a b)").bitcast(F32)]
            for layer, (w, a) in enumerate(((w0, a0), (w1, a1))):
                general_layer(nc, layer, x, adj, w, a, out, mem["x_sb"], mem["ident"], general_room, banks)


INPUTS = ["x", "adj", "L0_gnn_W", "L0_gnn_a", "L1_gnn_W", "L1_gnn_a"]


def kernel(**inputs):
    import numpy as np
    import concourse.bacc as bacc
    from concourse.bass_utils import run_bass_kernel_spmd

    nc = bacc.Bacc("TRN2", target_bir_lowering=False, num_devices=1)
    arrays, args = {}, []
    for name in INPUTS:
        arrays[f"in_{name}"] = np.ascontiguousarray(inputs[name])
        a = arrays[f"in_{name}"]
        args.append(nc.dram_tensor(f"in_{name}", a.shape, mybir.dt.from_np(a.dtype), kind="ExternalInput").ap())
    shape = inputs["x"].shape
    args.append(nc.dram_tensor("out_x", shape, F32, kind="ExternalOutput").ap())
    build(nc, *args)
    result = run_bass_kernel_spmd(nc, [arrays], core_ids=[0])
    return result.results[0]["out_x"]
```
